# Optimizing a Trainium2 kernel written in Bass

```python
import numpy as np
import jax
import jax.numpy as jnp

def _softmax(x, axis=-1):
    return jax.nn.softmax(x, axis=axis)

def _gelu(x):
    return jax.nn.gelu(x, approximate=True)

def _silu(x):
    return jax.nn.silu(x)

def _sigmoid(x):
    return jax.nn.sigmoid(x)

def _layernorm(x, axis=-1, eps=1e-05):
    m = jnp.mean(x, axis=axis, keepdims=True)
    v = jnp.var(x, axis=axis, keepdims=True)
    return (x - m) / jnp.sqrt(v + eps)

def _scatter_add(tgt, idx, src, axis=0):
    return tgt.at[idx].add(src)

def _segment_sum(src, seg, n):
    return jax.ops.segment_sum(src, seg, n)
kernel_name = 'mk_flamingo_gated_d1_seqx_r4_4a5adc'

def setup_inputs(seed: int=0):
    np.random.seed(seed)
    _w = jnp.asarray

    def _rec_inputs():
        import jax
        import jax.numpy as jnp
        _rk = jax.random.key(seed)
        x = -0.0003929 + 0.9999 * jax.random.normal(jax.random.fold_in(_rk, 1), (32, 128, 1024), jnp.float32)
        _lenS = 128 - jax.random.randint(jax.random.fold_in(_rk, 7), (32,), 0, max(1, 128 // 4) + 1, jnp.int32)
        _lenS2 = 128 - jax.random.randint(jax.random.fold_in(_rk, 8), (32,), 0, max(1, 128 // 4) + 1, jnp.int32)
        _ctx_4096P = jax.random.normal(jax.random.fold_in(_rk, 11), (32, 16, 1024), jnp.float32)
        _ctx_4096c = jax.random.dirichlet(jax.random.fold_in(_rk, 511), 0.3 * jnp.ones((16,), jnp.float32), (32, 128))
        _ctx_4096t = jnp.einsum('bsk,bkd->bsd', _ctx_4096c, _ctx_4096P)
        _ctx_4096t = _ctx_4096t * jax.lax.rsqrt(jnp.mean(jnp.square(_ctx_4096t)) + 1e-12) * 0.953939
        ctx_4096 = 2.81802e-05 + 1.00001 * (_ctx_4096t + 0.3 * jax.random.normal(jax.random.fold_in(_rk, 611), (32, 128, 1024), jnp.float32))
        _g = jax.random.normal(jax.random.fold_in(_rk, 9001), (2, 1), jnp.float32)
        _g = jnp.sign(_g) * jnp.maximum(jnp.abs(_g), 1.0) + (_g == 0) * 1.0
        g_xattn = _g[0]
        g_ffn = _g[1]
        return (x, ctx_4096, g_xattn, g_ffn)
    x, ctx_4096, g_xattn, g_ffn = _rec_inputs()

    def _L0_xattn_setup():
        import jax, jax.numpy as jnp
        import numpy as np
        EMBED = 1024
        NUM_Q = 32
        NUM_KV = 8
        GROUPS = NUM_Q // NUM_KV
        HEAD_DIM = EMBED // NUM_Q
        KV_DIM = HEAD_DIM * NUM_KV
        key = jax.random.key(seed)
        ks = jax.random.split(key, 12)
        B, S = (2, 512)
        s = 0.02
        return {'query': jax.random.normal(ks[0], (B, S, EMBED), jnp.float32), 'key': jax.random.normal(ks[1], (B, S, EMBED), jnp.float32), 'value': jax.random.normal(ks[2], (B, S, EMBED), jnp.float32), 'Wq': jax.random.normal(ks[3], (EMBED, EMBED), jnp.float32) * s, 'bq': jnp.zeros((EMBED,), jnp.float32), 'Wk': jax.random.normal(ks[4], (EMBED, KV_DIM), jnp.float32) * s, 'bk': jnp.zeros((KV_DIM,), jnp.float32), 'Wv': jax.random.normal(ks[5], (EMBED, KV_DIM), jnp.float32) * s, 'bv': jnp.zeros((KV_DIM,), jnp.float32), 'Wo': jax.random.normal(ks[6], (EMBED, EMBED), jnp.float32) * s, 'bo': jnp.zeros((EMBED,), jnp.float32)}
    _L0_xattn_all = _L0_xattn_setup()
    _L0_xattn_in = {k: v for k, v in _L0_xattn_all.items() if k in ('Wq', 'bq', 'Wk', 'bk', 'Wv', 'bv', 'Wo', 'bo')}
    del _L0_xattn_all

    def _L0_ffn_setup():
        import jax, jax.numpy as jnp
        import numpy as np
        LORA_RANK = 16
        LORA_ALPHA = 16
        LORA_SCALE = LORA_ALPHA / LORA_RANK
        key = jax.random.key(seed)
        k1, k2, k3, k4, k5 = jax.random.split(key, 5)
        B, S, D_IN, D_OUT, N_LORA, R = (8, 512, 1024, 1024, 3, LORA_RANK)
        std = 1.0 / np.sqrt(D_IN)
        x = jax.random.normal(k1, (B, S, D_IN), dtype=jnp.float32)
        weight = jax.random.truncated_normal(k2, -3.0, 3.0, (D_OUT, D_IN), dtype=jnp.float32) * std
        bias = jax.random.normal(k3, (D_OUT,), dtype=jnp.float32) * 0.01
        lora_A = jax.random.normal(k4, (N_LORA, R, D_IN), dtype=jnp.float32) * std
        lora_B = jax.random.normal(k5, (N_LORA, D_OUT, R), dtype=jnp.float32) * 0.02
        lora_start_indices = jnp.arange(4, dtype=jnp.int64) * 2
        return {'x': x, 'weight': weight, 'bias': bias, 'lora_A': lora_A, 'lora_B': lora_B, 'lora_start_indices': lora_start_indices}
    _L0_ffn_all = _L0_ffn_setup()
    _L0_ffn_in = {k: v for k, v in _L0_ffn_all.items() if k in ('weight', 'bias', 'lora_A', 'lora_B', 'lora_start_indices')}
    del _L0_ffn_all
    return {'x': x, 'ctx_4096': ctx_4096, 'g_xattn': g_xattn, 'g_ffn': g_ffn, 'L0_xattn_Wq': _L0_xattn_in['Wq'], 'L0_xattn_bq': _L0_xattn_in['bq'], 'L0_xattn_Wk': _L0_xattn_in['Wk'], 'L0_xattn_bk': _L0_xattn_in['bk'], 'L0_xattn_Wv': _L0_xattn_in['Wv'], 'L0_xattn_bv': _L0_xattn_in['bv'], 'L0_xattn_Wo': _L0_xattn_in['Wo'], 'L0_xattn_bo': _L0_xattn_in['bo'], 'L0_ffn_weight': _L0_ffn_in['weight'], 'L0_ffn_bias': _L0_ffn_in['bias'], 'L0_ffn_lora_A': _L0_ffn_in['lora_A'], 'L0_ffn_lora_B': _L0_ffn_in['lora_B'], 'L0_ffn_lora_start_indices': _L0_ffn_in['lora_start_indices']}

def reference(x, ctx_4096, g_xattn, g_ffn, L0_xattn_Wq, L0_xattn_bq, L0_xattn_Wk, L0_xattn_bk, L0_xattn_Wv, L0_xattn_bv, L0_xattn_Wo, L0_xattn_bo, L0_ffn_weight, L0_ffn_bias, L0_ffn_lora_A, L0_ffn_lora_B, L0_ffn_lora_start_indices):
    import jax
    import jax.numpy as jnp

    def _L0_xattn_ref(query, key, value, Wq, bq, Wk, bk, Wv, bv, Wo, bo):
        import jax, jax.numpy as jnp
        import numpy as np
        EMBED = 1024
        NUM_Q = 32
        NUM_KV = 8
        GROUPS = NUM_Q // NUM_KV
        HEAD_DIM = EMBED // NUM_Q
        KV_DIM = HEAD_DIM * NUM_KV
        B, S, _ = query.shape
        Q = query @ Wq + bq
        K = key @ Wk + bk
        V = value @ Wv + bv
        Q = Q.reshape(B, S, NUM_KV, GROUPS, HEAD_DIM).transpose(0, 2, 3, 1, 4)
        K = K.reshape(B, S, NUM_KV, HEAD_DIM).transpose(0, 2, 1, 3)
        V = V.reshape(B, S, NUM_KV, HEAD_DIM).transpose(0, 2, 1, 3)
        scale = 1.0 / jnp.sqrt(jnp.asarray(HEAD_DIM, query.dtype))
        scores = jnp.einsum('bhgqd,bhkd->bhgqk', Q, K) * scale
        w = jax.nn.softmax(scores, axis=-1)
        y = jnp.einsum('bhgqk,bhkd->bhgqd', w, V)
        y = y.transpose(0, 3, 1, 2, 4).reshape(B, S, EMBED)
        return y @ Wo + bo

    def _L0_ffn_ref(x, weight, bias, lora_A, lora_B, lora_start_indices):
        import jax, jax.numpy as jnp
        import numpy as np
        LORA_RANK = 16
        LORA_ALPHA = 16
        LORA_SCALE = LORA_ALPHA / LORA_RANK
        y = jnp.einsum('bsd,od->bso', x, weight) + bias
        B = x.shape[0]
        seg = jnp.searchsorted(lora_start_indices, jnp.arange(B), side='right') - 1
        adapter_idx = jnp.clip(seg - 1, 0, lora_A.shape[0] - 1)
        A = lora_A[adapter_idx]
        Bw = lora_B[adapter_idx]
        lo = jnp.einsum('bsr,bor->bso', jnp.einsum('bsd,brd->bsr', x, A), Bw) * LORA_SCALE
        use_lora = (seg > 0)[:, None, None]
        return y + jnp.where(use_lora, lo, jnp.zeros((), dtype=y.dtype))
    x = x + jnp.tanh(g_xattn[0]) * _L0_xattn_ref(_layernorm(x, axis=-1), ctx_4096, ctx_4096, L0_xattn_Wq, L0_xattn_bq, L0_xattn_Wk, L0_xattn_bk, L0_xattn_Wv, L0_xattn_bv, L0_xattn_Wo, L0_xattn_bo)
    x = x + jnp.tanh(g_ffn[0]) * _L0_ffn_ref(_layernorm(x, axis=-1), L0_ffn_weight, L0_ffn_bias, L0_ffn_lora_A, L0_ffn_lora_B, L0_ffn_lora_start_indices)
    return x

_drawn_inputs = setup_inputs


def setup_inputs(seed=0):
    import zlib

    import numpy as np

    out = dict(_drawn_inputs(seed))
    spreads = {'L0_xattn_bq': (0.0, 0.8),
     'L0_xattn_bk': (0.0, 0.8),
     'L0_xattn_bv': (0.0, 0.1),
     'L0_xattn_bo': (0.0, 0.1)}
    factors = {'L0_ffn_bias': 8.0}
    for name, (base, spread) in spreads.items():
        noise = np.random.default_rng([zlib.crc32(name.encode()), seed]).standard_normal(out[name].shape)
        drawn = base * np.exp(spread * noise) if base else spread * noise
        out[name] = jnp.asarray(drawn.astype(out[name].dtype))
    for name, factor in factors.items():
        out[name] = (out[name] * factor).astype(out[name].dtype)
    return out
```

```python
from contextlib import ExitStack

import concourse.bass as bass
from concourse import mybir

F32 = mybir.dt.float32
F32R = mybir.dt.float32r
I32 = mybir.dt.int32
ALU = mybir.AluOpType
ACT = mybir.ActivationFunctionType
AX_X = mybir.AxisListType.X

P = 128
BATCHES = 32
EMBED = 1024
KC = EMBED // P
NUM_KV = 8
GROUPS = 4
DH = 32
KVD = NUM_KV * DH
HALF = EMBED // 2
UNITS = 8
SCALE = float(DH) ** -0.5
EPS = 1e-5
ADAPTERS = 3
RANK = 16
LR = ADAPTERS * RANK
LO_ROW = 64
STACK = LO_ROW + LR
DMA = 16
TERMS = 3
GROUP_MM = KC * TERMS


class Batch:

    def __init__(self, offset, pair=0):
        self.n = pair * 2 + offset if not isinstance(pair, int) else 2 * pair + offset
        self.par = offset % 2
        self.earlier = pair + offset // 2
        self.pair, self.offset = pair, offset

    def __add__(self, k):
        return Batch(self.offset + k, self.pair)

    def exists(self):
        return not isinstance(self.n, int) or 0 <= self.n < BATCHES


def need(engine, semaphore, count):
    if not isinstance(count, int) or count > 0:
        engine.wait_ge(semaphore, count)


def unit_of(a, s):
    return (a, s) if s >= 0 else (a + (-1), s + UNITS)


def attention_phase(nc, x, ctx_in, wq, bq, wk, bk, wv, bv, at_dram):
    with ExitStack() as ctx:
        def sb(name, shape, dt=F32):
            return ctx.enter_context(nc.sbuf_tensor(name, shape, dt))

        def sem(name):
            return ctx.enter_context(nc.semaphore(name))

        bank = [ctx.enter_context(nc.psum_tensor(f"att_bank{i}", [P, HALF], F32)) for i in range(8)]
        score_ps, probsT_ps, mm_ps = bank[0:2], bank[2:4], bank[4:6]
        at_ps, turn_ps = bank[6], bank[7]

        wkv = [sb(f"wkv_{t}", [P, KC, 2 * KVD], F32R) for t in ("hi", "lo")]
        wqs = [sb(f"wq_{t}", [P, KC, EMBED], F32R) for t in ("hi", "lo")]
        ctxT = [[sb(f"ctxT{i}_{t}", [P, KC, P], F32R) for t in ("hi", "lo")] for i in range(2)]
        xT = [[sb(f"xT{i}_{t}", [P, KC, P], F32R) for t in ("hi", "lo")] for i in range(2)]
        qT = [sb(f"qT_{t}", [P, 2, GROUPS, P], F32R) for t in ("hi", "lo")]
        kD = [[sb(f"kD{i}_{t}", [P, 2, 4, P], F32R) for t in ("hi", "lo")] for i in range(2)]
        kv = [sb(f"kv{i}", [P, 2 * KVD]) for i in range(2)]
        q_sb = sb("q_sb", [P, 2, GROUPS, 4, DH])
        x_raw = [sb(f"x_raw{i}", [P, EMBED]) for i in range(2)]
        c_raw = [sb(f"c_raw{i}", [P, EMBED]) for i in range(2)]
        probs = [sb(f"probs{i}", [P, 4, P]) for i in range(4)]
        probsT = [sb(f"probsT{i}", [P, 4, P]) for i in range(2)]
        at_sb = [sb(f"at_sb{i}", [P, EMBED]) for i in range(2)]
        bq_row = sb("bq_row", [P, EMBED])
        bkv_row = sb("bkv_row", [P, 2 * KVD])
        ident = sb("ident", [P, P])
        row_max = sb("row_max", [P, UNITS, 4])
        neg_max = sb("neg_max", [P, UNITS, 4])
        row_sum = sb("row_sum", [P, UNITS, 4])
        inv_sum = sb("inv_sum", [P, UNITS, 4])
        stats = sb("stats", [P, 2, 6])
        mean_var = sb("mean_var", [P, 2])
        var_eps = sb("var_eps", [P, 1])
        rstd = sb("rstd", [P, 1])
        minus_half = sb("minus_half", [P, 1])

        raw_loaded = [sem(f"raw_loaded{i}") for i in range(2)]
        stage_loaded = [sem(f"stage_loaded{i}") for i in range(2)]
        biases_loaded = sem("biases_loaded")
        at_stored = [sem(f"at_stored{i}") for i in range(2)]
        ident_zeroed, ident_ready, kd_zeroed = sem("ident_zeroed"), sem("ident_ready"), sem("kd_zeroed")
        weight_hi, weight_lo = sem("weight_hi"), sem("weight_lo")
        turned = {k: sem(f"{k}_turned") for k in "cxqk"}
        hi_ready = {k: sem(f"{k}_hi") for k in "cxqk"}
        lo_ready = {k: sem(f"{k}_lo") for k in "cxqk"}
        projected, drained = sem("projected"), sem("drained")
        stats_ready, mean_ready, var_ready = sem("stats_ready"), sem("mean_ready"), sem("var_ready")
        rstd_ready, xn_ready = sem("rstd_ready"), sem("xn_ready")
        scored, row_max_ready, neg_max_ready = sem("scored"), sem("row_max_ready"), sem("neg_max_ready")
        exp_done, inv_ready, probs_ready = sem("exp_done"), sem("inv_ready"), sem("probs_ready")
        probs_turned = sem("probs_turned")
        probsT_ready = [sem("probsT_by_act"), sem("probsT_by_dve")]
        values_summed, at_ready = sem("values_summed"), sem("at_ready")

        PARTS = {"c": 2, "x": 2, "q": 2, "k": 1}

        def count(kind, b, part):
            return b.n * PARTS[kind] + part + 1

        def fills(a):
            return [("c", a + 2, 0), ("q", a, 1), ("c", a + 2, 1), None,
                    ("k", a + 1, 0), ("x", a + 2, 0), ("q", a + 1, 0), ("x", a + 2, 1)]

        def fill_before(a, s):
            for f in list(reversed(fills(a)[:s])) + list(reversed(fills(a + (-1)))):
                if f is not None and f[1].exists():
                    return f
            return None

        def fill_in(a, s):
            if s < 0:
                a, s = a + (-1), s + UNITS
            f = fills(a)[s]
            return f if f is not None and f[1].exists() else None

        KV_STAGES = KC // 2
        STAGES = KV_STAGES + KC

        def stage_count(w):
            kv_dmas = 2 * ((min(w, KV_STAGES - 2 + w % 2)) // 2 + 1)
            q_dmas = (w - KV_STAGES) // 2 + 1 if w >= KV_STAGES else 0
            return DMA * (kv_dmas + q_dmas)

        def stage_parts(w):
            if w < KV_STAGES:
                hi, lo = (t[:, 2 * w:2 * w + 2, :].rearrange("p k n -> p (k n)") for t in wkv)
            else:
                hi, lo = (t[:, w - KV_STAGES, :] for t in wqs)
            return at_sb[w % 2][:, :], hi, lo

        loop_pairs = 14
        before = [Batch(a) for a in (-2, -1, 0)]
        after = [Batch(a) for a in range(2 * loop_pairs + 1, BATCHES + 1)]

        def iterations(engine, body):
            for a in before[1:]:
                body(a)
            with engine.Fori(0, loop_pairs) as pair:
                body(Batch(1, pair))
                body(Batch(2, pair))
            for a in after:
                body(a)

        block = ctx.enter_context(nc.Block())

        @block.sync
        def _(sp):
            wk_v = wk.rearrange("(k p) n -> p k n", p=P)
            wv_v = wv.rearrange("(k p) n -> p k n", p=P)

            def load_raw(b):
                if not b.exists():
                    return
                need(sp, turned["c"], (b + (-2)).n * 2 + 2)
                need(sp, turned["x"], (b + (-2)).n * 2 + 2)
                sp.dma_start(c_raw[b.par][:, :], ctx_in[b.n]).then_inc(raw_loaded[b.par], DMA)
                sp.dma_start(x_raw[b.par][:, :], x[b.n]).then_inc(raw_loaded[b.par], DMA)

            def load_stage(w):
                if w >= 2:
                    sp.wait_ge(weight_lo, w - 1)
                tile = at_sb[w % 2]
                if w < KV_STAGES:
                    t = tile[:, :].rearrange("p (k n) -> p k n", k=2)
                    sp.dma_start(t[:, :, 0:KVD], wk_v[:, 2 * w:2 * w + 2, :]).then_inc(stage_loaded[w % 2], DMA)
                    sp.dma_start(t[:, :, KVD:], wv_v[:, 2 * w:2 * w + 2, :]).then_inc(stage_loaded[w % 2], DMA)
                else:
                    k = w - KV_STAGES
                    sp.dma_start(tile[:, :], wq[k * P:(k + 1) * P, :]).then_inc(stage_loaded[w % 2], DMA)

            load_raw(Batch(0))
            for w in range(2):
                load_stage(w)
            sp.dma_start(bkv_row[:, 0:KVD], bk.partition_broadcast(P)).then_inc(biases_loaded, DMA)
            sp.dma_start(bkv_row[:, KVD:], bv.partition_broadcast(P)).then_inc(biases_loaded, DMA)
            sp.dma_start(bq_row[:, :], bq.partition_broadcast(P)).then_inc(biases_loaded, DMA)
            for w in range(2, 6):
                load_stage(w)
            load_raw(Batch(1))
            for w in range(6, STAGES):
                load_stage(w)

            def body(a):
                load_raw(a + 3)
                b = a + (-1)
                if b.exists():
                    need(sp, at_ready, b.n * 2 + 2)
                    sp.dma_start(at_dram[b.n], at_sb[b.par][:, :]).then_inc(at_stored[b.par], DMA)

            iterations(sp, body)
            for i in range(2):
                sp.wait_ge(at_stored[i], DMA * (BATCHES // 2))

        @block.tensor
        def _(pe):
            def transposes(a, s):
                f = fill_in(a, s)
                if f is None:
                    return
                kind, b, part = f
                last = fill_before(a, s)
                if last is not None:
                    need(pe, lo_ready[last[0]], count(*last))
                if kind == "c":
                    need(pe, raw_loaded[b.par], (b.earlier + 1) * 2 * DMA)
                    src = [c_raw[b.par][:, k * P:(k + 1) * P] for k in range(4 * part, 4 * part + 4)]
                elif kind == "x":
                    need(pe, xn_ready, b.n + 1)
                    src = [x_raw[b.par][:, k * P:(k + 1) * P] for k in range(4 * part, 4 * part + 4)]
                elif kind == "q":
                    need(pe, drained, b.n * 3 + 2 + part)
                    src = [q_sb[:, part, j, :, :].rearrange("p q d -> p (q d)") for j in range(GROUPS)]
                else:
                    need(pe, drained, b.n * 3 + 1)
                    src = [kv[b.par][:, h * P:(h + 1) * P] for h in range(2)]
                for i, t in enumerate(src):
                    mm = nc.tensor.transpose(turn_ps[:, i * P:(i + 1) * P], t, ident[:, :])
                mm.then_inc(turned[kind], 1)

            def project(b, first, n):
                if not b.exists():
                    return
                for m in range(first, first + n):
                    g, r = divmod(m, GROUP_MM)
                    k, term = divmod(r, TERMS)
                    if r == 0:
                        src = "c" if g == 0 else "x"
                        if g < 2:
                            need(pe, lo_ready[src], count(src, b, 1))
                        need(pe, drained, b.n * 3 + g - 1)
                        if isinstance(b.n, int) and b.n == 0 and g < 2:
                            pe.wait_ge(weight_lo, KV_STAGES if g == 0 else STAGES)
                    act_t = (ctxT if g == 0 else xT)[b.par][term // 2]
                    w = wkv if g == 0 else wqs
                    rhs = w[term % 2][:, k, :] if g == 0 else w[term % 2][:, k, (g - 1) * HALF:g * HALF]
                    mm = nc.tensor.matmul(mm_ps[(g + b.par) % 2][:, :], act_t[:, k, :], rhs,
                                          start=(r == 0), stop=(r == GROUP_MM - 1))
                    if r == GROUP_MM - 1:
                        mm.then_inc(projected, 1)

            def scores(b, s):
                if not b.exists():
                    return
                half, j = divmod(s, GROUPS)
                if j == 0:
                    need(pe, lo_ready["q"], count("q", b, half))
                if s == 0:
                    need(pe, lo_ready["k"], count("k", b, 0))
                need(pe, exp_done, b.n * UNITS + s - 1)
                for term in range(TERMS):
                    mm = nc.tensor.matmul(
                        score_ps[s % 2][:, :], qT[term // 2][:, half, j, :],
                        kD[b.par][term % 2][:, half, :, :].rearrange("p q k -> p (q k)"),
                        start=(term == 0), stop=(term == TERMS - 1))
                mm.then_inc(scored, 1)

            def turn_probs(b, s):
                if not b.exists():
                    return
                need(pe, probs_ready, b.n * UNITS + s + 1)
                need(pe, probsT_ready[s % 2], b.n * 4 + s // 2)
                for q in range(4):
                    mm = nc.tensor.transpose(probsT_ps[s % 2][:, q * P:(q + 1) * P], probs[s % 4][:, q, :],
                                             ident[:, :])
                mm.then_inc(probs_turned, 1)

            def sum_values(b, s):
                if not b.exists():
                    return
                half, j = divmod(s, GROUPS)
                if j == 0:
                    need(pe, at_ready, b.n * 2 + half)
                need(pe, probsT_ready[s % 2], b.n * 4 + s // 2 + 1)
                for q in range(4):
                    v0 = KVD + (4 * half + q) * DH
                    mm = nc.tensor.matmul(at_ps[q * DH:(q + 1) * DH, j * P:(j + 1) * P],
                                          kv[b.par][:, v0:v0 + DH], probsT[s % 2][:, q, :],
                                          start=True, stop=True)
                mm.then_inc(values_summed, 1)

            def body(a):
                for s in range(UNITS):
                    scores(a, s)
                    sum_values(*unit_of(a, s - 3))
                    project(a + 1, 9 * s, 5)
                    turn_probs(*unit_of(a, s - 2))
                    project(a + 1, 9 * s + 5, 4)
                    transposes(a, s)

            pe.wait_ge(ident_ready, 1)
            body(before[0])
            iterations(pe, body)

        @block.scalar
        def _(act):
            def split_stage(w):
                src, hi, _ = stage_parts(w)
                act.wait_ge(stage_loaded[w % 2], stage_count(w))
                nc.scalar.activation(hi, src, ACT.Copy).then_inc(weight_hi, 1)

            def high_parts(a, s):
                f = fill_in(a, s)
                if f is None:
                    return
                kind, b, part = f
                need(act, turned[kind], count(*f))
                if kind == "k":
                    need(act, scored, b.n * UNITS - UNITS)
                    for q in range(4):
                        rows = slice(q * DH, (q + 1) * DH)
                        ins = nc.scalar.activation(
                            kD[b.par][0][rows, :, q, :],
                            turn_ps[rows, 0:2 * P].rearrange("p (h k) -> p h k", h=2), ACT.Copy)
                else:
                    if kind == "q":
                        dst = qT[0][:, part, :, :]
                        need(act, scored, b.n * UNITS - UNITS + 4 * part + 4)
                    else:
                        dst = (ctxT if kind == "c" else xT)[b.par][0][:, 4 * part:4 * part + 4, :]
                        need(act, projected, b.n * 3 - 6 + (1 if kind == "c" else 3))
                    ins = nc.scalar.activation(dst.rearrange("p k t -> p (k t)"), turn_ps[:, :], ACT.Copy)
                ins.then_inc(hi_ready[kind], 1)

            def exponentials(b, s):
                if not b.exists():
                    return
                need(act, neg_max_ready, b.n * UNITS + s + 1)
                need(act, probs_turned, b.n * UNITS + s - 3)
                for q in range(4):
                    ins = nc.scalar.activation(probs[s % 4][:, q, :], score_ps[s % 2][:, q * P:(q + 1) * P],
                                               ACT.Exp, bias=neg_max[:, s, q:q + 1], scale=SCALE,
                                               accum_out=row_sum[:, s, q:q + 1])
                ins.then_inc(exp_done, 1)

            def copy_probsT(b, s):
                if not b.exists() or s % 2:
                    return
                need(act, probs_turned, b.n * UNITS + s + 1)
                need(act, values_summed, b.n * UNITS + s - 1)
                nc.scalar.activation(probsT[0][:, :, :].rearrange("p q k -> p (q k)"), probsT_ps[0][:, :],
                                     ACT.Copy).then_inc(probsT_ready[0], 1)

            def body(a):
                for s in range(UNITS):
                    high_parts(a, s - 1)
                    exponentials(a, s)
                    copy_probsT(*unit_of(a, s - 2))

            for w in range(KV_STAGES):
                split_stage(w)
            body(before[0])
            for w in range(KV_STAGES, STAGES):
                split_stage(w)
            act.wait_ge(kd_zeroed, 4)
            iterations(act, body)

        @block.vector
        def _(dve):
            def split_stage(w):
                src, hi, lo = stage_parts(w)
                dve.wait_ge(weight_hi, w + 1)
                nc.vector.tensor_tensor(lo, src, hi, ALU.subtract).then_inc(weight_lo, 1)

            def low_parts(a, s):
                f = fill_in(a, s)
                if f is None:
                    return
                kind, b, part = f
                need(dve, hi_ready[kind], count(*f))
                if kind == "k":
                    for q in range(4):
                        rows = slice(q * DH, (q + 1) * DH)
                        hi, lo = (t[rows, :, q, :] for t in kD[b.par])
                        ins = nc.vector.tensor_tensor(
                            lo, turn_ps[rows, 0:2 * P].rearrange("p (h k) -> p h k", h=2), hi, ALU.subtract)
                else:
                    if kind == "q":
                        hi, lo = (t[:, part, :, :] for t in qT)
                    else:
                        hi, lo = (t[:, 4 * part:4 * part + 4, :] for t in (ctxT if kind == "c" else xT)[b.par])
                    hi, lo = (t.rearrange("p k t -> p (k t)") for t in (hi, lo))
                    ins = nc.vector.tensor_tensor(lo, turn_ps[:, :], hi, ALU.subtract)
                ins.then_inc(lo_ready[kind], 1)

            def drain(b, g):
                if not b.exists():
                    return
                need(dve, projected, b.n * 3 + g + 1)
                ps = mm_ps[(g + b.par) % 2]
                if g == 0:
                    need(dve, values_summed, b.n * UNITS - UNITS)
                    ins = nc.vector.tensor_tensor(kv[b.par][:, :], ps[:, :], bkv_row[:, :], ALU.add)
                else:
                    half = g - 1
                    need(dve, turned["q"], b.n * 2 - 1 + half)
                    order = "p (q j d) -> p q j d"
                    ins = nc.vector.tensor_tensor(
                        q_sb[:, half, :, :, :].rearrange("p j q d -> p q j d"),
                        ps[:, :].rearrange(order, q=4, j=GROUPS),
                        bq_row[:, half * HALF:(half + 1) * HALF].rearrange(order, q=4, j=GROUPS), ALU.add)
                ins.then_inc(drained, 1)

            def maxima(b, s):
                if not b.exists():
                    return
                need(dve, scored, b.n * UNITS + s + 1)
                nc.vector.tensor_reduce(row_max[:, s, :], score_ps[s % 2][:, :].rearrange("p (q k) -> p q k", q=4),
                                        AX_X, ALU.max).then_inc(row_max_ready, 1)
                need(dve, row_max_ready, b.n * UNITS + s + 1)
                nc.vector.tensor_scalar(neg_max[:, s, :], row_max[:, s, :], -SCALE, None,
                                        ALU.mult).then_inc(neg_max_ready, 1)

            def inverse_sums(b, s):
                if not b.exists():
                    return
                need(dve, exp_done, b.n * UNITS + s + 1)
                nc.vector.reciprocal(inv_sum[:, s, :], row_sum[:, s, :]).then_inc(inv_ready, 1)

            def copy_probsT(b, s):
                if not b.exists() or s % 2 == 0:
                    return
                need(dve, probs_turned, b.n * UNITS + s + 1)
                need(dve, values_summed, b.n * UNITS + s - 1)
                nc.vector.tensor_copy(probsT[1][:, :, :].rearrange("p q k -> p (q k)"),
                                      probsT_ps[1][:, :]).then_inc(probsT_ready[1], 1)

            def copy_at(b, s):
                half, j = divmod(s, GROUPS)
                if not b.exists() or j < GROUPS - 1:
                    return
                need(dve, values_summed, b.n * UNITS + s + 1)
                if half == 0:
                    need(dve, at_stored[b.par], b.earlier * DMA)
                nc.vector.tensor_copy(at_sb[b.par][:, half * HALF:(half + 1) * HALF],
                                      at_ps[:, :]).then_inc(at_ready, 1)

            def row_stats(b):
                if not b.exists():
                    return
                need(dve, raw_loaded[b.par], (b.earlier + 1) * 2 * DMA)
                for h in range(2):
                    nc.vector.bn_stats(stats[:, h, :], x_raw[b.par][:, h * HALF:(h + 1) * HALF]).then_inc(stats_ready, 1)

            def inverse_std_input(b):
                if not b.exists():
                    return
                nc.vector.bn_aggr(mean_var[:, :], stats[:, :, :].rearrange("p h s -> p (h s)")).then_inc(mean_ready, 1)
                need(dve, mean_ready, b.n + 1)
                nc.vector.tensor_scalar(var_eps[:, :], mean_var[:, 1:2], EPS, None, ALU.add).then_inc(var_ready, 1)

            def normalise(b):
                if not b.exists():
                    return
                need(dve, rstd_ready, b.n + 1)
                nc.vector.tensor_scalar(x_raw[b.par][:, :], x_raw[b.par][:, :], mean_var[:, 0:1], rstd[:, 0:1],
                                        ALU.subtract, ALU.mult).then_inc(xn_ready, 1)

            def body(a):
                for s in range(UNITS):
                    if s == 2 and (a + 2).exists():
                        need(dve, stats_ready, (a + 2).n * 2 + 2)
                    maxima(a, s)
                    if s == 2:
                        inverse_std_input(a + 2)
                    if s == 0:
                        drain(a, 2)
                    if s == 3:
                        drain(a + 1, 0)
                    if s == 6:
                        drain(a + 1, 1)
                    low_parts(a, s - 1)
                    inverse_sums(*unit_of(a, s - 1))
                    copy_probsT(*unit_of(a, s - 2))
                    copy_at(*unit_of(a, s - 3))
                    if s == 1:
                        row_stats(a + 2)
                    if s == 3:
                        normalise(a + 2)

            for i in range(2):
                for t in kD[i]:
                    nc.vector.memset(t[:, :, :, :].bitcast(F32), 0.0).then_inc(kd_zeroed, 1)
            dve.wait_ge(kd_zeroed, 4)
            for w in range(KV_STAGES):
                split_stage(w)
            body(before[0])
            for w in range(KV_STAGES, STAGES):
                split_stage(w)
            dve.wait_ge(biases_loaded, 3 * DMA)
            iterations(dve, body)

        @block.gpsimd
        def _(pool):
            nc.gpsimd.memset(ident[:, :], 0.0).then_inc(ident_zeroed, 1)
            nc.gpsimd.memset(minus_half[:, :], -0.5).then_inc(ident_zeroed, 1)
            pool.wait_ge(ident_zeroed, 2)
            nc.gpsimd.affine_select(out=ident[:, :], in_=ident[:, :], compare_op=ALU.not_equal, fill=1.0,
                                    base=0, pattern=[[-1, P]], channel_multiplier=1).then_inc(ident_ready, 1)

            def inverse_std(b):
                if not b.exists():
                    return
                need(pool, var_ready, b.n + 1)
                nc.gpsimd.tensor_tensor(rstd[:, :], var_eps[:, :], minus_half[:, :], ALU.pow).then_inc(rstd_ready, 1)

            def divide(b, s):
                if not b.exists():
                    return
                need(pool, inv_ready, b.n * UNITS + s + 1)
                nc.gpsimd.tensor_tensor(probs[s % 4][:, :, :], probs[s % 4][:, :, :],
                                        inv_sum[:, s, :].unsqueeze(2).broadcast_to([P, 4, P]),
                                        ALU.mult).then_inc(probs_ready, 1)

            def body(a):
                for s in range(UNITS):
                    divide(*unit_of(a, s - 1))
                    if s == 2:
                        inverse_std(a + 2)

            body(before[0])
            iterations(pool, body)


def ffn_phase(nc, x, g_xattn, g_ffn, wo, bo, w_t, bias, lora_a_t, lora_b_t, starts, at_dram, out):
    with ExitStack() as ctx:
        def sb(name, shape, dt=F32):
            return ctx.enter_context(nc.sbuf_tensor(name, shape, dt))

        def sem(name):
            return ctx.enter_context(nc.semaphore(name))

        bank = [ctx.enter_context(nc.psum_tensor(f"ffn_bank{i}", [P, HALF], F32)) for i in range(8)]
        o_ps, f_ps, turn_ps = bank[0:2], bank[2:4], bank[4:6]
        u_ps = bank[6:8]

        wos = [sb(f"wo_{t}", [P, KC, EMBED], F32R) for t in ("hi", "lo")]
        wfs = [sb(f"wf_{t}", [P, KC, EMBED], F32R) for t in ("hi", "lo")]
        lb_hi = sb("lb_hi", [STACK, EMBED], F32R)
        lb_lo = sb("lb_lo", [LR + 1, EMBED], F32R)
        la = sb("la", [P, KC, LR])
        at_raw = [sb(f"at_raw{i}", [P, EMBED]) for i in range(2)]
        x_in = [sb(f"x_in{i}", [P, EMBED]) for i in range(2)]
        atT = [[sb(f"atT{i}_{t}", [P, KC, P], F32R) for t in ("hi", "lo")] for i in range(2)]
        x1 = [sb(f"x1_{i}", [P, EMBED]) for i in range(2)]
        x2T = [sb(f"x2T_{t}", [P, KC, P], F32R) for t in ("hi", "lo")]
        x2T_full = sb("x2T_full", [P, KC, P])
        out_sb = [sb(f"out_sb{i}", [P, EMBED]) for i in range(2)]
        bo_row = sb("bo_row", [P, EMBED])
        gates = sb("gates", [P, 2])
        tanhs = sb("tanhs", [P, 2])
        starts_i = sb("starts_i", [P, ADAPTERS + 1], I32)
        starts_f = sb("starts_f", [P, ADAPTERS + 1])
        batch_i = sb("batch_i", [P, BATCHES], I32)
        batch_f = sb("batch_f", [P, BATCHES])
        begun = sb("begun", [P, BATCHES])
        row_i = sb("row_i", [P, 1], I32)
        row_f = sb("row_f", [P, 1])
        row_step = sb("row_step", [P, 1])
        begun_at = sb("begun_at", [P, 1])
        mask = sb("mask", [P, BATCHES])
        u_odd = sb("u_odd", [LR, P])
        u_sb = sb("u_sb", [LR, P])
        uT = sb("uT", [STACK, P], F32R)
        ident = sb("ident2", [P, P])
        stats = sb("stats2", [P, 2, 6])
        mean_var = sb("mean_var2", [P, 2])
        var_eps = sb("var_eps2", [P, 1])
        rstd = sb("rstd2", [P, 1])
        minus_half = sb("minus_half2", [P, 1])

        loaded = [sem(f"loaded{i}") for i in range(2)]
        stage_loaded = [sem(f"w_stage_loaded{i}") for i in range(2)]
        small_loaded, gates_ready, bo_scaled = sem("small_loaded"), sem("gates_ready"), sem("bo_scaled")
        lb_zeroed, lb_loaded, lb_hi_ready, lb_lo_ready = (sem(n) for n in ("lb_zeroed", "lb_loaded", "lb_hi_ready", "lb_lo_ready"))
        ident_zeroed, ident_ready, batch_ready = sem("ident_zeroed2"), sem("ident_ready2"), sem("batch_ready")
        mask_steps, stack_set = sem("mask_steps"), sem("stack_set")
        weight_hi, weight_lo = sem("w_hi"), sem("w_lo")
        at_hi, at_lo, x_biased = sem("at_hi"), sem("at_lo"), sem("x_biased")
        o_done, x1_ready = sem("o_done"), sem("x1_ready")
        stats_ready, mean_ready, var_ready, rstd_ready, x2_ready = (
            sem(n) for n in ("stats_ready2", "mean_ready2", "var_ready2", "rstd_ready2", "x2_ready"))
        x2_turned, x2_hi, x2_full, x2_lo = sem("x2_turned"), sem("x2_hi"), sem("x2_full"), sem("x2_lo")
        u_done, u_odd_ready, u_ready, u_hi, u_lo = (
            sem(n) for n in ("u_done", "u_odd_ready", "u_ready", "u_hi", "u_lo"))
        f_done, out_ready = sem("f_done"), sem("out_ready")
        out_stored = [sem(f"out_stored{i}") for i in range(2)]

        STAGES = 2 * KC
        loop_pairs = 14
        before = [Batch(a) for a in (-2, -1, 0)]
        after = [Batch(a) for a in range(2 * loop_pairs + 1, BATCHES)]

        def iterations(engine, body):
            for i in before:
                body(i)
            with engine.Fori(0, loop_pairs) as pair:
                body(Batch(1, pair))
                body(Batch(2, pair))
            for i in after:
                body(i)

        def stage_parts(w):
            tiles = wos if w < KC else wfs
            return (out_sb[w % 2][:, :], *(t[:, w % KC, :] for t in tiles))

        block = ctx.enter_context(nc.Block())

        @block.sync
        def _(sp):
            wo_v = wo.rearrange("(h q j d) n -> h j q d n", h=2, q=4, j=GROUPS)

            def load(b):
                if not b.exists():
                    return
                need(sp, at_lo, b.n - 1)
                need(sp, x1_ready, b.n * 2 - 2)
                sp.dma_start(at_raw[b.par][:, :], at_dram[b.n]).then_inc(loaded[b.par], DMA)
                sp.dma_start(x_in[b.par][:, :], x[b.n]).then_inc(loaded[b.par], DMA)

            def load_stage(w):
                if w >= 2:
                    sp.wait_ge(weight_lo, w - 1)
                if w < KC:
                    for q in range(4):
                        sp.dma_start(out_sb[w % 2][q * DH:(q + 1) * DH, :],
                                     wo_v[w // 4, w % 4, q]).then_inc(stage_loaded[w % 2], DMA)
                else:
                    k = w - KC
                    sp.dma_start(out_sb[w % 2][:, :], w_t[k * P:(k + 1) * P, :]).then_inc(stage_loaded[w % 2], DMA)

            for dst, src in ((gates[:, 0:1], g_xattn), (gates[:, 1:2], g_ffn), (bo_row[:, :], bo),
                             (starts_i[:, :], starts)):
                sp.dma_start(dst, src.partition_broadcast(P)).then_inc(small_loaded, DMA)
            sp.dma_start(la[:, :, :], lora_a_t.rearrange("(k p) r -> p k r", p=P)).then_inc(small_loaded, DMA)
            load_stage(0)
            load_stage(1)
            sp.wait_ge(lb_zeroed, 1)
            sp.dma_start(x1[0][0:LR, :], lora_b_t).then_inc(lb_loaded, DMA)
            sp.dma_start(x1[0][LR:LR + 1, :], bias.unsqueeze(0)).then_inc(lb_loaded, DMA)
            sp.dma_start(x1[0][LO_ROW:STACK, :], lora_b_t).then_inc(lb_loaded, DMA)
            load(Batch(0))
            for w in range(2, STAGES):
                load_stage(w)

            def body(i):
                load(i + 3)
                if i.exists():
                    need(sp, out_ready, i.n * 2 + 2)
                    sp.dma_start(out[i.n], out_sb[i.par][:, :]).then_inc(out_stored[i.par], DMA)

            iterations(sp, body)
            for i in range(2):
                sp.wait_ge(out_stored[i], DMA * (BATCHES // 2))

        def stage_count(w):
            wo_dmas = 4 * (min(w, KC - 2 + w % 2) // 2 + 1)
            return DMA * (wo_dmas + ((w - KC) // 2 + 1 if w >= KC else 0))

        @block.tensor
        def _(pe):
            def group(ps, b, g, act_t, w, extra):
                for r in range(GROUP_MM):
                    k, term = divmod(r, TERMS)
                    mm = nc.tensor.matmul(ps[:, :], act_t[term // 2][:, k, :],
                                          w[term % 2][:, k, g * HALF:(g + 1) * HALF],
                                          start=(r == 0), stop=(r == GROUP_MM - 1 and not extra))
                if extra:
                    need(pe, u_lo, b.n + 1)
                    cols = slice(g * HALF, (g + 1) * HALF)
                    nc.tensor.matmul(ps[:, :], uT[:, :], lb_hi[:, cols], start=False, stop=False)
                    mm = nc.tensor.matmul(ps[:, :], uT[0:LR + 1, :], lb_lo[:, cols], start=False, stop=True)
                return mm

            def out_projection(b, g):
                if not b.exists():
                    return
                need(pe, at_lo, b.n + 1)
                need(pe, x1_ready, b.n * 2 + g - 1)
                group(o_ps[g], b, g, atT[b.par], wos, False).then_inc(o_done, 1)

            def feed_forward(b, g):
                if not b.exists():
                    return
                need(pe, x2_lo, b.n * 2 + 2)
                need(pe, out_ready, b.n * 2 + g - 1)
                group(f_ps[g], b, g, x2T, wfs, True).then_inc(f_done, 1)

            def turn_x2(b):
                if not b.exists():
                    return
                need(pe, x2_ready, b.n + 1)
                for f in range(2):
                    need(pe, x2_lo, b.n * 2 + f - 1)
                    need(pe, x2_full, b.n * 2 + f - 1)
                    for i in range(4):
                        k = 4 * f + i
                        mm = nc.tensor.transpose(turn_ps[f][:, i * P:(i + 1) * P],
                                                 out_sb[b.par][:, k * P:(k + 1) * P], ident[:, :])
                    mm.then_inc(x2_turned, 1)

            def lora_down(b):
                if not b.exists():
                    return
                need(pe, x2_full, b.n * 2 + 2)
                need(pe, u_ready, b.n)
                for k in range(KC):
                    row = LO_ROW * (k % 2)
                    mm = nc.tensor.matmul(u_ps[k % 2][row:row + LR, 0:P], la[:, k, :], x2T_full[:, k, :],
                                          start=(k < 2), stop=(k >= KC - 2))
                mm.then_inc(u_done, 1)

            def body(i):
                out_projection(i + 1, 0)
                lora_down(i)
                out_projection(i + 1, 1)
                feed_forward(i, 0)
                feed_forward(i, 1)
                turn_x2(i + 1)

            pe.wait_ge(ident_ready, 1)
            pe.wait_ge(small_loaded, 5 * DMA)
            pe.wait_ge(lb_lo_ready, 1)
            pe.wait_ge(weight_lo, STAGES)
            iterations(pe, body)

        @block.scalar
        def _(act):
            act.wait_ge(small_loaded, 5 * DMA)
            nc.scalar.activation(tanhs[:, :], gates[:, :], ACT.Tanh).then_inc(gates_ready, 1)
            act.wait_ge(lb_loaded, 3 * DMA)
            nc.scalar.activation(lb_hi[:, :], x1[0][0:STACK, :], ACT.Copy).then_inc(lb_hi_ready, 1)
            for w in range(STAGES):
                src, hi, _ = stage_parts(w)
                act.wait_ge(stage_loaded[w % 2], stage_count(w))
                nc.scalar.activation(hi, src, ACT.Copy).then_inc(weight_hi, 1)

            def high_at(b):
                if not b.exists():
                    return
                need(act, loaded[b.par], (b.earlier + 1) * 2 * DMA)
                need(act, o_done, b.n * 2 - 2)
                nc.scalar.activation(atT[b.par][0][:, :, :].rearrange("p k t -> p (k t)"), at_raw[b.par][:, :],
                                     ACT.Copy).then_inc(at_hi, 1)

            def high_x2(b):
                if not b.exists():
                    return
                need(act, f_done, b.n * 2)
                need(act, u_done, b.n)
                for f in range(2):
                    need(act, x2_turned, b.n * 2 + f + 1)
                    part = slice(4 * f, 4 * f + 4)
                    nc.scalar.activation(x2T[0][:, part, :].rearrange("p k t -> p (k t)"), turn_ps[f][:, :],
                                         ACT.Copy).then_inc(x2_hi, 1)
                    nc.scalar.activation(x2T_full[:, part, :].rearrange("p k t -> p (k t)"), turn_ps[f][:, :],
                                         ACT.Copy).then_inc(x2_full, 1)

            def body(i):
                high_at(i + 2)
                high_x2(i + 1)

            iterations(act, body)

        @block.vector
        def _(dve):
            nc.vector.memset(x1[0][:, :], 0.0).then_inc(lb_zeroed, 1)
            dve.wait_ge(small_loaded, 5 * DMA)
            dve.wait_ge(batch_ready, 2)
            nc.vector.tensor_copy(starts_f[:, :], starts_i[:, :]).then_inc(mask_steps, 1)
            nc.vector.tensor_copy(batch_f[:, :], batch_i[:, :]).then_inc(mask_steps, 1)
            nc.vector.tensor_copy(row_f[:, :], row_i[:, :]).then_inc(mask_steps, 1)
            dve.wait_ge(mask_steps, 3)
            nc.vector.tensor_scalar(begun[:, :], batch_f[:, :], starts_f[:, 0:1], None, ALU.is_ge).then_inc(mask_steps, 1)
            for k in range(1, ADAPTERS + 1):
                dve.wait_ge(mask_steps, 3 + k)
                nc.vector.scalar_tensor_tensor(out=begun[:, :], in0=batch_f[:, :], scalar=starts_f[:, k:k + 1],
                                               in1=begun[:, :], op0=ALU.is_ge, op1=ALU.add).then_inc(mask_steps, 1)
            dve.wait_ge(mask_steps, 4 + ADAPTERS)
            nc.vector.tensor_scalar(uT[LO_ROW // 2:LO_ROW, :],
                                    row_f[LO_ROW // 2:LO_ROW, 0:1].broadcast_to([LO_ROW // 2, P]), float(LR), None,
                                    ALU.is_equal).then_inc(stack_set, 1)
            dve.wait_ge(stack_set, 1)
            nc.vector.tensor_scalar(begun_at[:, :], row_f[:, :], float(RANK), 2.0, ALU.is_ge, ALU.add).then_inc(mask_steps, 1)
            steps = 5 + ADAPTERS
            for at_row, by in ((2 * RANK, 1.0), (LO_ROW, -2.0), (LO_ROW + RANK, 1.0), (LO_ROW + 2 * RANK, 1.0)):
                dve.wait_ge(mask_steps, steps)
                nc.vector.tensor_scalar(row_step[:, :], row_f[:, :], float(at_row), by, ALU.is_ge,
                                        ALU.mult).then_inc(mask_steps, 1)
                dve.wait_ge(mask_steps, steps + 1)
                nc.vector.tensor_tensor(begun_at[:, :], begun_at[:, :], row_step[:, :], ALU.add).then_inc(mask_steps, 1)
                steps += 2
            dve.wait_ge(mask_steps, steps)
            nc.vector.tensor_scalar(mask[:, :], begun[:, :], float(ADAPTERS + 1), begun_at[:, 0:1], ALU.min,
                                    ALU.is_equal).then_inc(mask_steps, 1)
            dve.wait_ge(gates_ready, 1)
            nc.vector.tensor_scalar(bo_row[:, :], bo_row[:, :], tanhs[:, 0:1], None, ALU.mult).then_inc(bo_scaled, 1)
            dve.wait_ge(lb_hi_ready, 1)
            nc.vector.tensor_tensor(lb_lo[:, :], x1[0][0:LR + 1, :], lb_hi[0:LR + 1, :],
                                    ALU.subtract).then_inc(lb_lo_ready, 1)
            for w in range(STAGES):
                src, hi, lo = stage_parts(w)
                dve.wait_ge(weight_hi, w + 1)
                nc.vector.tensor_tensor(lo, src, hi, ALU.subtract).then_inc(weight_lo, 1)
            dve.wait_ge(mask_steps, steps + 1)
            dve.wait_ge(lb_lo_ready, 1)

            def attended(b, g):
                if not b.exists():
                    return
                cols = slice(g * HALF, (g + 1) * HALF)
                need(dve, o_done, b.n * 2 + g + 1)
                need(dve, x_biased, b.n + 1)
                need(dve, out_ready, b.n * 2 - 2)
                nc.vector.scalar_tensor_tensor(out=x1[b.par][:, cols], in0=o_ps[g][:, :], scalar=tanhs[:, 0:1],
                                               in1=x_in[b.par][:, cols], op0=ALU.mult,
                                               op1=ALU.add).then_inc(x1_ready, 1)

            def norm(b):
                if not b.exists():
                    return
                for h in range(2):
                    need(dve, x1_ready, b.n * 2 + h + 1)
                    nc.vector.bn_stats(stats[:, h, :], x1[b.par][:, h * HALF:(h + 1) * HALF]).then_inc(stats_ready, 1)
                dve.wait_ge(mask_steps, 3)
                need(dve, stats_ready, b.n * 2 + 2)
                nc.vector.bn_aggr(mean_var[:, :], stats[:, :, :].rearrange("p h s -> p (h s)")).then_inc(mean_ready, 1)
                need(dve, mean_ready, b.n + 1)
                nc.vector.tensor_scalar(var_eps[:, :], mean_var[:, 1:2], EPS, None, ALU.add).then_inc(var_ready, 1)
                need(dve, rstd_ready, b.n + 1)
                need(dve, out_stored[b.par], b.earlier * DMA)
                nc.vector.tensor_scalar(out_sb[b.par][:, :], x1[b.par][:, :], mean_var[:, 0:1], rstd[:, 0:1],
                                        ALU.subtract, ALU.mult).then_inc(x2_ready, 1)

            def outputs(b, g):
                if not b.exists():
                    return
                cols = slice(g * HALF, (g + 1) * HALF)
                need(dve, f_done, b.n * 2 + g + 1)
                nc.vector.scalar_tensor_tensor(out=out_sb[b.par][:, cols], in0=f_ps[g][:, :], scalar=tanhs[:, 1:2],
                                               in1=x1[b.par][:, cols], op0=ALU.mult,
                                               op1=ALU.add).then_inc(out_ready, 1)

            def low_x2(b):
                if not b.exists():
                    return
                for f in range(2):
                    need(dve, x2_full, b.n * 2 + f + 1)
                    hi, lo = (t[:, 4 * f:4 * f + 4, :].rearrange("p k t -> p (k t)") for t in x2T)
                    nc.vector.tensor_tensor(lo, turn_ps[f][:, :], hi, ALU.subtract).then_inc(x2_lo, 1)

            def split_u(b):
                if not b.exists():
                    return
                need(dve, u_done, b.n + 1)
                nc.vector.tensor_scalar(u_odd[:, :], u_ps[1][LO_ROW:STACK, 0:P], mask[LO_ROW:STACK, bass.ds(b.n, 1)], None,
                                        ALU.mult).then_inc(u_odd_ready, 1)
                need(dve, u_odd_ready, b.n + 1)
                nc.vector.scalar_tensor_tensor(out=u_sb[:, :], in0=u_ps[0][0:LR, 0:P], scalar=mask[0:LR, bass.ds(b.n, 1)],
                                               in1=u_odd[:, :], op0=ALU.mult, op1=ALU.add).then_inc(u_ready, 1)
                need(dve, u_ready, b.n + 1)
                need(dve, f_done, b.n * 2)
                nc.vector.tensor_copy(uT[0:LR, :], u_sb[:, :]).then_inc(u_hi, 1)
                need(dve, u_hi, b.n + 1)
                nc.vector.tensor_tensor(uT[LO_ROW:STACK, :], u_sb[:, :], uT[0:LR, :], ALU.subtract).then_inc(u_lo, 1)

            def body(i):
                attended(i + 1, 0)
                split_u(i)
                attended(i + 1, 1)
                norm(i + 1)
                outputs(i, 0)
                outputs(i, 1)
                low_x2(i + 1)

            iterations(dve, body)

        @block.gpsimd
        def _(pool):
            nc.gpsimd.memset(ident[:, :], 0.0).then_inc(ident_zeroed, 1)
            nc.gpsimd.memset(minus_half[:, :], -0.5).then_inc(ident_zeroed, 1)
            pool.wait_ge(ident_zeroed, 2)
            nc.gpsimd.affine_select(out=ident[:, :], in_=ident[:, :], compare_op=ALU.not_equal, fill=1.0,
                                    base=0, pattern=[[-1, P]], channel_multiplier=1).then_inc(ident_ready, 1)
            nc.gpsimd.iota(batch_i[:, :], pattern=[[1, BATCHES]], base=0, channel_multiplier=0).then_inc(batch_ready, 1)
            nc.gpsimd.iota(row_i[:, :], pattern=[[0, 1]], base=0, channel_multiplier=1).then_inc(batch_ready, 1)
            pool.wait_ge(bo_scaled, 1)

            def low_at_and_bias(b):
                if not b.exists():
                    return
                need(pool, at_hi, b.n + 1)
                hi, lo = (t[:, :, :].rearrange("p k t -> p (k t)") for t in atT[b.par])
                nc.gpsimd.tensor_tensor(lo, at_raw[b.par][:, :], hi, ALU.subtract).then_inc(at_lo, 1)
                nc.gpsimd.tensor_tensor(x_in[b.par][:, :], x_in[b.par][:, :], bo_row[:, :],
                                        ALU.add).then_inc(x_biased, 1)

            def inverse_std(b):
                if not b.exists():
                    return
                need(pool, var_ready, b.n + 1)
                nc.gpsimd.tensor_tensor(rstd[:, :], var_eps[:, :], minus_half[:, :], ALU.pow).then_inc(rstd_ready, 1)

            def body(i):
                low_at_and_bias(i + 2)
                inverse_std(i + 1)

            iterations(pool, body)


def build_program(nc, x, ctx_in, g_xattn, g_ffn, wq, bq, wk, bk, wv, bv, wo, bo, w_t, bias, lora_a_t, lora_b_t,
                  starts, out):
    at_dram = nc.dram_tensor("attention_out", (BATCHES, P, EMBED), F32).ap()
    attention_phase(nc, x, ctx_in, wq, bq, wk, bk, wv, bv, at_dram)
    ffn_phase(nc, x, g_xattn, g_ffn, wo, bo, w_t, bias, lora_a_t, lora_b_t, starts, at_dram, out)


def kernel(x, ctx_4096, g_xattn, g_ffn, L0_xattn_Wq, L0_xattn_bq, L0_xattn_Wk, L0_xattn_bk, L0_xattn_Wv,
           L0_xattn_bv, L0_xattn_Wo, L0_xattn_bo, L0_ffn_weight, L0_ffn_bias, L0_ffn_lora_A, L0_ffn_lora_B,
           L0_ffn_lora_start_indices):
    import numpy as np
    import concourse.bacc as bacc
    from concourse.bass_utils import run_bass_kernel_spmd

    nc = bacc.Bacc("TRN2", target_bir_lowering=False, num_devices=1)
    lora_b = np.asarray(L0_ffn_lora_B)
    ins = {
        "x": x, "ctx": ctx_4096, "g_xattn": g_xattn, "g_ffn": g_ffn,
        "wq": L0_xattn_Wq, "bq": L0_xattn_bq, "wk": L0_xattn_Wk, "bk": L0_xattn_bk,
        "wv": L0_xattn_Wv, "bv": L0_xattn_bv, "wo": L0_xattn_Wo, "bo": L0_xattn_bo,
        "w_t": np.asarray(L0_ffn_weight).T, "bias": L0_ffn_bias,
        "lora_a_t": np.asarray(L0_ffn_lora_A).reshape(-1, EMBED).T,
        "lora_b_t": lora_b.transpose(0, 2, 1).reshape(-1, EMBED),
        "starts": L0_ffn_lora_start_indices,
    }
    arrays, args = {}, []
    for name, a in ins.items():
        a = np.ascontiguousarray(a)
        arrays[f"in_{name}"] = a
        args.append(nc.dram_tensor(f"in_{name}", a.shape, mybir.dt.from_np(a.dtype), kind="ExternalInput").ap())
    args.append(nc.dram_tensor("out_x", (BATCHES, P, EMBED), F32, kind="ExternalOutput").ap())
    build_program(nc, *args)
    r = run_bass_kernel_spmd(nc, [arrays], core_ids=[0])
    return r.results[0]["out_x"]
```

```python
from contextlib import ExitStack

import concourse.bass as bass
from concourse import mybir

F32 = mybir.dt.float32
F32R = mybir.dt.float32r
I32 = mybir.dt.int32
ALU = mybir.AluOpType
ACT = mybir.ActivationFunctionType
AX_X = mybir.AxisListType.X

P = 128
BATCHES = 32
EMBED = 1024
KC = EMBED // P
NUM_KV = 8
GROUPS = 4
DH = 32
KVD = NUM_KV * DH
HALF = EMBED // 2
UNITS = 8
SCALE = float(DH) ** -0.5
EPS = 1e-5
ADAPTERS = 3
RANK = 16
LR = ADAPTERS * RANK
LO_ROW = 64
STACK = LO_ROW + LR
DMA = 16
TERMS = 3
GROUP_MM = KC * TERMS


class Batch:

    def __init__(self, offset, pair=0):
        self.n = pair * 2 + offset if not isinstance(pair, int) else 2 * pair + offset
        self.par = offset % 2
        self.earlier = pair + offset // 2
        self.pair, self.offset = pair, offset

    def __add__(self, k):
        return Batch(self.offset + k, self.pair)

    def exists(self):
        return not isinstance(self.n, int) or 0 <= self.n < BATCHES

    def at(self, n):
        return isinstance(self.n, int) and self.n == n


def need(engine, semaphore, count):
    if not isinstance(count, int) or count > 0:
        engine.wait_ge(semaphore, count)


def unit_of(a, s):
    return (a, s) if s >= 0 else (a + (-1), s + UNITS)


def flat(t):
    return t.rearrange("p a b -> p (a b)") if len(t.shape) == 3 else t.rearrange("p a b c -> p (a b c)")


class Shared:

    def __init__(self, nc, ctx):
        def sb(name, shape, dt=F32):
            return ctx.enter_context(nc.sbuf_tensor(name, shape, dt))

        self.wide = [sb(f"wide_{t}", [P, KC, EMBED], F32R) for t in ("hi", "lo")]
        self.raw_c = [sb(f"raw_c{i}", [P, EMBED]) for i in range(2)]
        self.raw_x = [sb(f"raw_x{i}", [P, EMBED]) for i in range(2)]
        self.ident = sb("ident", [P, P])
        self.ident_r = sb("ident_r", [P, P], F32R)
        self.minus_half = sb("minus_half", [P, 1])
        self.wo_loaded = [ctx.enter_context(nc.semaphore(f"wo_loaded{i}")) for i in range(4)]
        self.wo_hi = ctx.enter_context(nc.semaphore("wo_hi_ready"))
        self.wo_lo = ctx.enter_context(nc.semaphore("wo_lo_ready"))

    def wo_stage(self, w):
        return (self.raw_c + self.raw_x)[w % 4]


def attention_phase(nc, shared, x, ctx_in, wq, bq, wk, bk, wv, bv, wo, at_dram):
    with ExitStack() as ctx:
        def sb(name, shape, dt=F32):
            return ctx.enter_context(nc.sbuf_tensor(name, shape, dt))

        def sem(name):
            return ctx.enter_context(nc.semaphore(name))

        bank = [ctx.enter_context(nc.psum_tensor(f"att_bank{i}", [P, HALF], F32)) for i in range(8)]
        score_ps, mm_ps, at_ps, turn_ps = bank[0:2], bank[2:4], bank[4], bank[5:8]

        wkv = [sb(f"wkv_{t}", [P, KC, 2 * KVD], F32R) for t in ("hi", "lo")]
        wqs = shared.wide
        c_raw, x_raw, ident, minus_half = shared.raw_c, shared.raw_x, shared.ident, shared.minus_half
        ctxT = [sb(f"ctxT_{t}", [P, KC, P], F32R) for t in ("hi", "lo")]
        xT = [sb(f"xT_{t}", [P, KC, P], F32R) for t in ("hi", "lo")]
        q_sb = sb("q_sb", [P, 2, GROUPS, 4 * DH])
        q_halves = sb("q_halves", [P, 2, GROUPS * 4, 2, DH], F32R)
        qT = sb("qT", [P, 2, GROUPS * 2, P], F32R)
        k_twice = [sb(f"k_twice_{t}", [P, NUM_KV, 2, DH], F32R) for t in ("hi", "lo")]
        kD = [[sb(f"kD{i}_{t}", [P, NUM_KV // 2, 2, P], F32R) for t in ("hi", "lo")] for i in range(2)]
        k_sb = sb("k_sb", [P, KVD])
        values = [sb(f"values{i}", [P, KVD]) for i in range(2)]
        probs_all = sb("probs_all", [P, 4, 4, P])
        probs = [probs_all[:, i] for i in range(4)]
        probsT = [sb(f"probsT{i}", [P, 4, P]) for i in range(2)]
        at_sb = [sb(f"at_sb{i}", [P, EMBED]) for i in range(2)]
        bq_row = sb("bq_row", [P, EMBED])
        bkv_row = sb("bkv_row", [P, 2 * KVD])
        row_max = sb("row_max", [P, UNITS, 4])
        neg_max = sb("neg_max", [P, UNITS, 4])
        row_sum = sb("row_sum", [P, UNITS, 4])
        inv_sum = sb("inv_sum", [P, UNITS, 4])
        stats = sb("stats", [P, 2, 6])
        mean_var = sb("mean_var", [P, 2])
        var_eps = sb("var_eps", [P, 1])
        rstd = sb("rstd", [P, 1])

        c_loaded = [sem(f"c_loaded{i}") for i in range(2)]
        x_loaded = [sem(f"x_loaded{i}") for i in range(2)]
        stage_loaded = [sem(f"stage_loaded{i}") for i in range(4)]
        biases_loaded = sem("biases_loaded")
        at_stored = [sem(f"at_stored{i}") for i in range(2)]
        ident_zeroed, ident_ready, ident_r_ready = sem("ident_zeroed"), sem("ident_ready"), sem("ident_r_ready")
        kd_zeroed = sem("kd_zeroed")
        weight_hi, weight_lo = sem("weight_hi"), sem("weight_lo")
        turned = {k: sem(f"{k}_turned") for k in "cxqk"}
        hi_ready = {k: sem(f"{k}T_hi") for k in "cx"}
        lo_ready = {k: sem(f"{k}T_lo") for k in "cx"}
        qT_by_act, qT_by_dve = sem("qT_by_act"), sem("qT_by_dve")
        kD_by_act, kD_by_dve = sem("kD_by_act"), sem("kD_by_dve")
        q_hi_ready, q_lo_ready, k_hi_ready, k_lo_ready = (
            sem(n) for n in ("q_hi_ready", "q_lo_ready", "k_hi_ready", "k_lo_ready"))
        projected, drained, keys_drained = sem("projected"), sem("drained"), sem("keys_drained")
        stats_ready, mean_ready, var_ready = sem("stats_ready"), sem("mean_ready"), sem("var_ready")
        rstd_ready, xn_ready = sem("rstd_ready"), sem("xn_ready")
        scored, row_max_ready, neg_max_ready = sem("scored"), sem("row_max_ready"), sem("neg_max_ready")
        exp_done, inv_ready, probs_ready = sem("exp_done"), sem("inv_ready"), sem("probs_ready")
        probs_turned = sem("probs_turned")
        probsT_ready = [sem("probsT_by_act"), sem("probsT_by_dve")]
        values_summed, at_ready = sem("values_summed"), sem("at_ready")

        PARTS = {"c": 2, "x": 2, "q": 4, "k": 2}

        def count(kind, b, part):
            return b.n * PARTS[kind] + part + 1

        def left_bank(kind, b, part):
            if kind in "cx":
                return lo_ready[kind], count(kind, b, part)
            if kind == "q":
                return (qT_by_act, qT_by_dve)[part % 2], b.n * 2 + part // 2 + 1
            if kind == "p":
                return probsT_ready[part % 2], b.n * 4 + part // 2 + 1
            return (kD_by_act, kD_by_dve)[part], b.n + 1

        def fills(a):
            return [(None, ("c", a + 2, 0)), (None, ("q", a, 2)), (None, ("q", a, 3)),
                    (("k", a + 1, 0), ("c", a + 2, 1)), (None, ("k", a + 1, 1)), (None, ("q", a + 1, 0)),
                    (("q", a + 1, 1), ("x", a + 2, 0)), (None, ("x", a + 2, 1))]

        def fill_in(a, s, late):
            if s < 0:
                a, s = a + (-1), s + UNITS
            f = fills(a)[s][late]
            return f if f is not None and f[1].exists() else None

        PLACES = [(s, step) for s in range(UNITS) for step in range(3)
                  if step == 1 or fills(Batch(0))[s][step // 2] is not None]

        def turn_bank(s, step):
            return turn_ps[PLACES.index((s % UNITS, step)) % len(turn_ps)]

        def bank_before(a, s, step):
            place = PLACES.index((s, step)) - len(turn_ps)
            for _ in range(2 * len(PLACES)):
                it, at = (a, place) if place >= 0 else (a + (-1), place + len(PLACES))
                if at < 0:
                    return None
                s, step = PLACES[at]
                if step == 1:
                    b, unit = unit_of(it, s - 2)
                    f = ("p", b, unit)
                else:
                    f = fills(it)[s][step // 2]
                if f[1].exists():
                    return f
                place -= len(turn_ps)
            return None

        def group_of(a, m):
            i, r = divmod(m, GROUP_MM)
            return (a + 1, i + 1, r) if i < 2 else (a + 2, 0, r)

        def mm_bank(b, g):
            return mm_ps[(b.par + g) % 2]

        KV_STAGES = KC // 2
        STAGES = KV_STAGES + KC
        stage_tiles = [at_sb[0][:, :], at_sb[1][:, :]] + [
            probs_all[:, 2 * i:2 * i + 2].rearrange("p u q k -> p (u q k)") for i in range(2)]

        def stage_count(w):
            return 2 * DMA + DMA * (w // 4)

        def stage_parts(w):
            if w < KV_STAGES:
                hi, lo = (flat(t[:, 2 * w:2 * w + 2, :]) for t in wkv)
            else:
                hi, lo = (t[:, w - KV_STAGES, :] for t in wqs)
            return stage_tiles[w % 4], hi, lo

        def twice(keys):
            return keys[:, :].rearrange("p (g d) -> p g d", d=DH).unsqueeze(2).broadcast_to(
                [P, NUM_KV, 2, DH])

        loop_pairs = 14
        before = [Batch(a) for a in (-2, -1, 0)]
        after = [Batch(a) for a in range(2 * loop_pairs + 1, BATCHES + 1)]
        WO_ITERATION = BATCHES - 1

        def iterations(engine, body):
            for a in before[1:]:
                body(a)
            with engine.Fori(0, loop_pairs) as pair:
                body(Batch(1, pair))
                body(Batch(2, pair))
            for a in after:
                body(a)

        block = ctx.enter_context(nc.Block())

        @block.sync
        def _(sp):
            wk_v = wk.rearrange("(k p) n -> p k n", p=P)
            wv_v = wv.rearrange("(k p) n -> p k n", p=P)
            wo_v = wo.rearrange("(h q j d) n -> h j q d n", h=2, q=4, j=GROUPS)

            def load_c(b):
                if b.exists():
                    need(sp, turned["c"], (b + (-2)).n * 2 + 2)
                    sp.dma_start(c_raw[b.par][:, :], ctx_in[b.n]).then_inc(c_loaded[b.par], DMA)

            def load_x(b):
                if b.exists():
                    need(sp, turned["x"], (b + (-2)).n * 2 + 2)
                    sp.dma_start(x_raw[b.par][:, :], x[b.n]).then_inc(x_loaded[b.par], DMA)

            def load_stage(w):
                if w >= 4:
                    sp.wait_ge(weight_lo, w - 3)
                tile = stage_tiles[w % 4]
                if w < KV_STAGES:
                    t = tile.rearrange("p (k n) -> p k n", k=2)
                    sp.dma_start(t[:, :, 0:KVD], wk_v[:, 2 * w:2 * w + 2, :]).then_inc(stage_loaded[w % 4], DMA)
                    sp.dma_start(t[:, :, KVD:], wv_v[:, 2 * w:2 * w + 2, :]).then_inc(stage_loaded[w % 4], DMA)
                else:
                    k = w - KV_STAGES
                    sp.dma_start(tile, wq[k * P:(k + 1) * P, :]).then_inc(stage_loaded[w % 4], DMA)

            def load_wo(w):
                for q in range(4):
                    sp.dma_start(shared.wo_stage(w)[q * DH:(q + 1) * DH, :],
                                 wo_v[w // 4, w % 4, q]).then_inc(shared.wo_loaded[w % 4], DMA)

            load_c(Batch(0))
            for w in range(KV_STAGES):
                load_stage(w)
            load_x(Batch(0))
            sp.dma_start(bkv_row[:, 0:KVD], bk.partition_broadcast(P)).then_inc(biases_loaded, DMA)
            sp.dma_start(bkv_row[:, KVD:], bv.partition_broadcast(P)).then_inc(biases_loaded, DMA)
            sp.dma_start(bq_row[:, :], bq.partition_broadcast(P)).then_inc(biases_loaded, DMA)
            for w in range(KV_STAGES, STAGES):
                load_stage(w)
            load_c(Batch(1))
            load_x(Batch(1))

            def body(a):
                load_x(a + 3)
                load_c(a + 3)
                b = a + (-1)
                if b.exists():
                    need(sp, at_ready, b.n * 2 + 2)
                    sp.dma_start(at_dram[b.n], at_sb[b.par][:, :]).then_inc(at_stored[b.par], DMA)
                if a.at(WO_ITERATION - 1):
                    sp.wait_ge(turned["c"], BATCHES * 2)
                    sp.wait_ge(turned["x"], BATCHES * 2)
                    for w in range(4):
                        load_wo(w)
                if a.at(WO_ITERATION):
                    for w in range(4, KC):
                        sp.wait_ge(shared.wo_lo, w - 3)
                        load_wo(w)

            iterations(sp, body)
            for i in range(2):
                sp.wait_ge(at_stored[i], DMA * (BATCHES // 2))

        @block.tensor
        def _(pe):
            def bank_left(a, s, step):
                last = bank_before(a, s, step)
                if last is not None:
                    need(pe, *left_bank(*last))

            def transposes(a, s, late):
                f = fill_in(a, s, late)
                if f is None:
                    return
                kind, b, part = f
                bank_left(a, s, 2 * late)
                if kind == "c":
                    need(pe, c_loaded[b.par], (b.earlier + 1) * DMA)
                    src = [c_raw[b.par][:, k * P:(k + 1) * P] for k in range(4 * part, 4 * part + 4)]
                elif kind == "x":
                    need(pe, xn_ready, b.n + 1)
                    src = [x_raw[b.par][:, k * P:(k + 1) * P] for k in range(4 * part, 4 * part + 4)]
                elif kind == "q":
                    half, c0 = part // 2, part % 2 * 4
                    need(pe, q_lo_ready, b.n * 2 + half + 1)
                    src = [q_halves[:, half, 2 * c:2 * c + 2].rearrange("p q t d -> p (q t d)")
                           for c in range(c0, c0 + 4)]
                else:
                    need(pe, (k_hi_ready, k_lo_ready)[part], b.n + 1)
                    src = [k_twice[part][:, 2 * c:2 * c + 2].rearrange("p q t d -> p (q t d)") for c in range(4)]
                for i, t in enumerate(src):
                    dst = turn_bank(s, 2 * late)[:, i * P:(i + 1) * P]
                    if kind in "cx":
                        mm = nc.tensor.transpose(dst, t, ident[:, :])
                    else:
                        mm = nc.tensor.transpose(dst.bitcast(F32R), t, shared.ident_r[:, :])
                mm.then_inc(turned[kind], 1)

            def project(a, first, n):
                for m in range(first, first + n):
                    b, g, r = group_of(a, m)
                    if not b.exists():
                        continue
                    k, term = divmod(r, TERMS)
                    if r in (0, GROUP_MM // 2) and g < 2:
                        src = "x" if g else "c"
                        need(pe, lo_ready[src], count(src, b, int(r > 0)))
                    if r == 0:
                        need(pe, drained, b.n * 3 + g - 1)
                        if b.at(0) and g < 2:
                            pe.wait_ge(weight_lo, STAGES if g else KV_STAGES)
                    act_t = (xT if g else ctxT)[term // 2]
                    rhs = wqs[term % 2][:, k, (g - 1) * HALF:g * HALF] if g else wkv[term % 2][:, k, :]
                    mm = nc.tensor.matmul(mm_bank(b, g)[:, :], act_t[:, k, :], rhs,
                                          start=(r == 0), stop=(r == GROUP_MM - 1))
                    if r == GROUP_MM - 1:
                        mm.then_inc(projected, 1)

            def scores(b, s):
                if not b.exists():
                    return
                half, j = divmod(s, GROUPS)
                if j % 2 == 0:
                    need(pe, *left_bank("q", b, 2 * half + j // 2))
                if s == 0:
                    for part in range(2):
                        need(pe, *left_bank("k", b, part))
                need(pe, exp_done, b.n * UNITS + s - 1)
                for pair in range(2):
                    for t in range(2):
                        mm = nc.tensor.matmul(
                            score_ps[s % 2][:, pair * 2 * P:(pair + 1) * 2 * P], qT[:, half, 2 * j + pair, :],
                            kD[b.par][t][:, 2 * half + pair].rearrange("p q k -> p (q k)"),
                            start=(t == 0), stop=(t == 1))
                mm.then_inc(scored, 1)

            def turn_probs(a, slot):
                b, s = unit_of(a, slot - 2)
                if not b.exists():
                    return
                need(pe, probs_ready, b.n * UNITS + s + 1)
                bank_left(a, slot, 1)
                for q in range(4):
                    mm = nc.tensor.transpose(turn_bank(slot, 1)[:, q * P:(q + 1) * P], probs[s % 4][:, q, :],
                                             ident[:, :])
                mm.then_inc(probs_turned, 1)

            def sum_values(b, s):
                if not b.exists():
                    return
                half, j = divmod(s, GROUPS)
                if j == 0:
                    need(pe, at_ready, b.n * 2 + half)
                need(pe, probsT_ready[s % 2], b.n * 4 + s // 2 + 1)
                for q in range(4):
                    v0 = (4 * half + q) * DH
                    mm = nc.tensor.matmul(at_ps[q * DH:(q + 1) * DH, j * P:(j + 1) * P],
                                          values[b.par][:, v0:v0 + DH], probsT[s % 2][:, q, :],
                                          start=True, stop=True)
                mm.then_inc(values_summed, 1)

            def body(a):
                for s in range(UNITS):
                    scores(a, s)
                    if s % 2 == 0:
                        sum_values(*unit_of(a, s - 4))
                        sum_values(*unit_of(a, s - 3))
                    project(a, 9 * s, 5)
                    transposes(a, s, 0)
                    turn_probs(a, s)
                    project(a, 9 * s + 5, 4)
                    transposes(a, s, 1)

            pe.wait_ge(ident_ready, 1)
            pe.wait_ge(ident_r_ready, 1)
            body(before[0])
            iterations(pe, body)

        @block.scalar
        def _(act):
            def split_stage(w):
                src, hi, _ = stage_parts(w)
                act.wait_ge(stage_loaded[w % 4], stage_count(w))
                nc.scalar.activation(hi, src, ACT.Copy).then_inc(weight_hi, 1)

            def split_wo(w):
                act.wait_ge(shared.wo_loaded[w % 4], 4 * DMA * (w // 4 + 1))
                act.wait_ge(projected, 3 * BATCHES)
                nc.scalar.activation(shared.wide[0][:, w, :], shared.wo_stage(w)[:, :],
                                     ACT.Copy).then_inc(shared.wo_hi, 1)

            def take_turned(a, s, late):
                f = fill_in(a, s, late)
                if f is None:
                    return
                kind, b, part = f
                if kind in "qk" and part % 2:
                    return
                need(act, turned[kind], count(*f))
                ps = turn_bank(s, 2 * late)
                if kind == "k":
                    need(act, scored, b.n * UNITS - UNITS)
                    for h in range(2):
                        rows = slice(h * 2 * DH, (h + 1) * 2 * DH)
                        ins = nc.scalar.activation(
                            kD[b.par][0][rows, :, h, :],
                            ps[rows, :].rearrange("p (c k) -> p c k", c=4), ACT.Copy)
                    ins.then_inc(kD_by_act, 1)
                elif kind == "q":
                    half = part // 2
                    need(act, scored, b.n * UNITS - UNITS + 4 * half + 2)
                    nc.scalar.activation(flat(qT[:, half, 0:4, :]), ps[:, :], ACT.Copy).then_inc(qT_by_act, 1)
                else:
                    need(act, projected, b.n * 3 - 2 if kind == "c" else b.n * 3)
                    dst = (ctxT if kind == "c" else xT)[0][:, 4 * part:4 * part + 4, :]
                    nc.scalar.activation(flat(dst), ps[:, :], ACT.Copy).then_inc(hi_ready[kind], 1)

            def query_highs(b, half):
                if not b.exists():
                    return
                need(act, drained, b.n * 3 + half + 2)
                need(act, turned["q"], b.n * 4 - 2 + 2 * half)
                nc.scalar.activation(q_halves[:, half, :, 0, :],
                                     flat(q_sb[:, half:half + 1]).rearrange("p (q d) -> p q d", d=DH),
                                     ACT.Copy).then_inc(q_hi_ready, 1)

            def key_highs(b):
                if not b.exists():
                    return
                need(act, keys_drained, b.n + 1)
                need(act, turned["k"], b.n * 2)
                nc.scalar.activation(k_twice[0][:, :, :, :], twice(k_sb), ACT.Copy).then_inc(k_hi_ready, 1)

            def exponentials(b, s):
                if not b.exists():
                    return
                need(act, neg_max_ready, b.n * UNITS + s + 1)
                need(act, probs_turned, b.n * UNITS + s - 3)
                for q in range(4):
                    ins = nc.scalar.activation(probs[s % 4][:, q, :], score_ps[s % 2][:, q * P:(q + 1) * P],
                                               ACT.Exp, bias=neg_max[:, s, q:q + 1], scale=SCALE,
                                               accum_out=row_sum[:, s, q:q + 1])
                ins.then_inc(exp_done, 1)

            def copy_probsT(a, slot):
                b, s = unit_of(a, slot - 2)
                if not b.exists() or s % 2:
                    return
                need(act, probs_turned, b.n * UNITS + s + 1)
                need(act, values_summed, b.n * UNITS + s - 1)
                nc.scalar.activation(flat(probsT[0][:, :, :]), turn_bank(slot, 1)[:, :],
                                     ACT.Copy).then_inc(probsT_ready[0], 1)

            def body(a):
                for s in range(UNITS):
                    take_turned(a, s - 1, 1)
                    exponentials(a, s)
                    take_turned(a, s, 0)
                    copy_probsT(a, s)
                    if s == 1:
                        key_highs(a + 1)
                    if s == 4:
                        query_highs(a + 1, 0)
                    if s == 7:
                        query_highs(a + 1, 1)
                    if a.at(WO_ITERATION):
                        split_wo(s)

            for w in range(KV_STAGES):
                split_stage(w)
            body(before[0])
            for w in range(KV_STAGES, STAGES):
                split_stage(w)
            act.wait_ge(kd_zeroed, 4)
            iterations(act, body)

        @block.vector
        def _(dve):
            def split_stage(w):
                src, hi, lo = stage_parts(w)
                dve.wait_ge(weight_hi, w + 1)
                nc.vector.tensor_tensor(lo, src, hi, ALU.subtract).then_inc(weight_lo, 1)

            def split_wo(w):
                dve.wait_ge(shared.wo_hi, w + 1)
                hi, lo = (t[:, w, :] for t in shared.wide)
                nc.vector.tensor_tensor(lo, shared.wo_stage(w)[:, :], hi, ALU.subtract).then_inc(shared.wo_lo, 1)

            def take_turned(a, s, late):
                f = fill_in(a, s, late)
                if f is None:
                    return
                kind, b, part = f
                if kind in "qk" and part % 2 == 0:
                    return
                ps = turn_bank(s, 2 * late)
                if kind == "k":
                    need(dve, turned["k"], count(*f))
                    need(dve, scored, b.n * UNITS - UNITS)
                    for h in range(2):
                        rows = slice(h * 2 * DH, (h + 1) * 2 * DH)
                        ins = nc.vector.tensor_copy(
                            kD[b.par][1][rows, :, h, :],
                            ps[rows, :].rearrange("p (c k) -> p c k", c=4))
                    ins.then_inc(kD_by_dve, 1)
                elif kind == "q":
                    half = part // 2
                    need(dve, turned["q"], count(*f))
                    need(dve, scored, b.n * UNITS - UNITS + 4 * half + 4)
                    nc.vector.tensor_copy(flat(qT[:, half, 4:8, :]), ps[:, :]).then_inc(qT_by_dve, 1)
                else:
                    need(dve, hi_ready[kind], count(*f))
                    hi, lo = (flat(t[:, 4 * part:4 * part + 4, :]) for t in (ctxT if kind == "c" else xT))
                    nc.vector.tensor_tensor(lo, ps[:, :], hi, ALU.subtract).then_inc(lo_ready[kind], 1)

            def drain_keys(b):
                if not b.exists():
                    return
                need(dve, projected, b.n * 3 + 1)
                need(dve, k_lo_ready, b.n)
                nc.vector.tensor_tensor(k_sb[:, :], mm_bank(b, 0)[:, 0:KVD], bkv_row[:, 0:KVD],
                                        ALU.add).then_inc(keys_drained, 1)

            def drain(b, g):
                if not b.exists():
                    return
                need(dve, projected, b.n * 3 + g + 1)
                ps = mm_bank(b, g)
                if g == 0:
                    need(dve, values_summed, b.n * UNITS - UNITS)
                    ins = nc.vector.tensor_tensor(values[b.par][:, :], ps[:, KVD:], bkv_row[:, KVD:], ALU.add)
                else:
                    half = g - 1
                    need(dve, q_lo_ready, b.n * 2 - 1 + half)
                    order = "p (q j d) -> p q j d"
                    ins = nc.vector.tensor_tensor(
                        q_sb[:, half].rearrange("p j (q d) -> p q j d", d=DH),
                        ps[:, :].rearrange(order, q=4, j=GROUPS),
                        bq_row[:, half * HALF:(half + 1) * HALF].rearrange(order, q=4, j=GROUPS), ALU.add)
                ins.then_inc(drained, 1)

            def maxima(b, s):
                if not b.exists():
                    return
                need(dve, scored, b.n * UNITS + s + 1)
                nc.vector.tensor_reduce(row_max[:, s, :], score_ps[s % 2][:, :].rearrange("p (q k) -> p q k", q=4),
                                        AX_X, ALU.max).then_inc(row_max_ready, 1)
                need(dve, row_max_ready, b.n * UNITS + s + 1)
                nc.vector.tensor_scalar(neg_max[:, s, :], row_max[:, s, :], -SCALE, None,
                                        ALU.mult).then_inc(neg_max_ready, 1)

            def inverse_sums(b, s):
                if not b.exists():
                    return
                need(dve, exp_done, b.n * UNITS + s + 1)
                nc.vector.reciprocal(inv_sum[:, s, :], row_sum[:, s, :]).then_inc(inv_ready, 1)

            def copy_probsT(a, slot):
                b, s = unit_of(a, slot - 2)
                if not b.exists() or s % 2 == 0:
                    return
                need(dve, probs_turned, b.n * UNITS + s + 1)
                need(dve, values_summed, b.n * UNITS + s - 1)
                nc.vector.tensor_copy(flat(probsT[1][:, :, :]), turn_bank(slot, 1)[:, :]).then_inc(probsT_ready[1], 1)

            def copy_at(b, s):
                half, j = divmod(s, GROUPS)
                if not b.exists() or j < GROUPS - 1:
                    return
                need(dve, values_summed, b.n * UNITS + s + 1)
                if half == 0:
                    need(dve, at_stored[b.par], b.earlier * DMA)
                nc.vector.tensor_copy(at_sb[b.par][:, half * HALF:(half + 1) * HALF],
                                      at_ps[:, :]).then_inc(at_ready, 1)

            def row_stats(b):
                if not b.exists():
                    return
                need(dve, x_loaded[b.par], (b.earlier + 1) * DMA)
                for h in range(2):
                    nc.vector.bn_stats(stats[:, h, :], x_raw[b.par][:, h * HALF:(h + 1) * HALF]).then_inc(stats_ready, 1)

            def variance(b):
                if not b.exists():
                    return
                nc.vector.bn_aggr(mean_var[:, :], flat(stats[:, :, :])).then_inc(mean_ready, 1)
                need(dve, mean_ready, b.n + 1)
                nc.vector.tensor_scalar(var_eps[:, :], mean_var[:, 1:2], EPS, None, ALU.add).then_inc(var_ready, 1)

            def normalise(b):
                if not b.exists():
                    return
                need(dve, rstd_ready, b.n + 1)
                nc.vector.tensor_scalar(x_raw[b.par][:, :], x_raw[b.par][:, :], mean_var[:, 0:1], rstd[:, 0:1],
                                        ALU.subtract, ALU.mult).then_inc(xn_ready, 1)

            def body(a):
                for s in range(UNITS):
                    if s == 4 and (a + 2).exists():
                        need(dve, stats_ready, (a + 2).n * 2 + 2)
                    maxima(a, s)
                    if s == 2:
                        drain(a + 1, 0)
                    take_turned(a, s - 1, 1)
                    inverse_sums(*unit_of(a, s - 1))
                    if s == 4:
                        variance(a + 2)
                    copy_at(*unit_of(a, s - 3))
                    if s == 0:
                        drain_keys(a + 1)
                    if s == 3:
                        drain(a + 1, 1)
                    if s == 6:
                        drain(a + 1, 2)
                    take_turned(a, s, 0)
                    copy_probsT(a, s)
                    if s == 3:
                        row_stats(a + 2)
                    if s == 5:
                        normalise(a + 2)
                    if a.at(WO_ITERATION):
                        split_wo(s)

            for i in range(2):
                for t in kD[i]:
                    nc.vector.memset(t[:, :, :, :].bitcast(F32), 0.0).then_inc(kd_zeroed, 1)
            dve.wait_ge(ident_ready, 1)
            nc.vector.tensor_copy(shared.ident_r[:, :], ident[:, :]).then_inc(ident_r_ready, 1)
            dve.wait_ge(kd_zeroed, 4)
            for w in range(KV_STAGES):
                split_stage(w)
            body(before[0])
            for w in range(KV_STAGES, STAGES):
                split_stage(w)
            dve.wait_ge(biases_loaded, 3 * DMA)
            iterations(dve, body)

        @block.gpsimd
        def _(pool):
            nc.gpsimd.memset(ident[:, :], 0.0).then_inc(ident_zeroed, 1)
            nc.gpsimd.memset(minus_half[:, :], -0.5).then_inc(ident_zeroed, 1)
            pool.wait_ge(ident_zeroed, 2)
            nc.gpsimd.affine_select(out=ident[:, :], in_=ident[:, :], compare_op=ALU.not_equal, fill=1.0,
                                    base=0, pattern=[[-1, P]], channel_multiplier=1).then_inc(ident_ready, 1)

            def inverse_std(b):
                if not b.exists():
                    return
                need(pool, var_ready, b.n + 1)
                nc.gpsimd.tensor_tensor(rstd[:, :], var_eps[:, :], minus_half[:, :], ALU.pow).then_inc(rstd_ready, 1)

            def divide(b, s):
                if not b.exists():
                    return
                need(pool, inv_ready, b.n * UNITS + s + 1)
                nc.gpsimd.tensor_tensor(probs[s % 4][:, :, :], probs[s % 4][:, :, :],
                                        inv_sum[:, s, :].unsqueeze(2).broadcast_to([P, 4, P]),
                                        ALU.mult).then_inc(probs_ready, 1)

            def query_lows(b, half):
                if not b.exists():
                    return
                need(pool, q_hi_ready, b.n * 2 + half + 1)
                nc.gpsimd.tensor_tensor(q_halves[:, half, :, 1, :],
                                        flat(q_sb[:, half:half + 1]).rearrange("p (q d) -> p q d", d=DH),
                                        q_halves[:, half, :, 0, :], ALU.subtract).then_inc(q_lo_ready, 1)

            def key_lows(b):
                if not b.exists():
                    return
                need(pool, k_hi_ready, b.n + 1)
                nc.gpsimd.tensor_tensor(k_twice[1][:, :, :, :], twice(k_sb), k_twice[0][:, :, :, :],
                                        ALU.subtract).then_inc(k_lo_ready, 1)

            def body(a):
                for s in range(UNITS):
                    divide(*unit_of(a, s - 1))
                    if s == 2:
                        key_lows(a + 1)
                    if s == 4:
                        inverse_std(a + 2)
                        query_lows(a + 1, 0)
                    if s == 7:
                        query_lows(a + 1, 1)

            body(before[0])
            iterations(pool, body)


def ffn_phase(nc, shared, x, g_xattn, g_ffn, bo, w_t, bias, lora_a_t, lora_b_t, starts, at_dram, out):
    with ExitStack() as ctx:
        def sb(name, shape, dt=F32):
            return ctx.enter_context(nc.sbuf_tensor(name, shape, dt))

        def sem(name):
            return ctx.enter_context(nc.semaphore(name))

        bank = [ctx.enter_context(nc.psum_tensor(f"ffn_bank{i}", [P, HALF], F32)) for i in range(8)]
        o_ps, f_ps, turn_ps = bank[0:2], bank[2:4], bank[4:6]
        u_ps = bank[6:8]

        wos, ident, minus_half = shared.wide, shared.ident, shared.minus_half
        wfs = [sb(f"wf_{t}", [P, KC, EMBED], F32R) for t in ("hi", "lo")]
        lb_hi = sb("lb_hi", [STACK, EMBED], F32R)
        lb_lo = sb("lb_lo", [LR + 1, EMBED], F32R)
        la = sb("la", [P, KC, LR])
        at_raw, x_in = shared.raw_c, shared.raw_x
        atT = [[sb(f"atT{i}_{t}", [P, KC, P], F32R) for t in ("hi", "lo")] for i in range(2)]
        x1 = [sb(f"x1_{i}", [P, EMBED]) for i in range(2)]
        x2T = [sb(f"x2T_{t}", [P, KC, P], F32R) for t in ("hi", "lo")]
        x2T_full = sb("x2T_full", [P, KC, P])
        out_sb = [sb(f"out_sb{i}", [P, EMBED]) for i in range(2)]
        bo_row = sb("bo_row", [P, EMBED])
        gates = sb("gates", [P, 2])
        tanhs = sb("tanhs", [P, 2])
        starts_i = sb("starts_i", [P, ADAPTERS + 1], I32)
        starts_f = sb("starts_f", [P, ADAPTERS + 1])
        batch_i = sb("batch_i", [P, BATCHES], I32)
        batch_f = sb("batch_f", [P, BATCHES])
        begun = sb("begun", [P, BATCHES])
        row_i = sb("row_i", [P, 1], I32)
        row_f = sb("row_f", [P, 1])
        row_step = sb("row_step", [P, 1])
        begun_at = sb("begun_at", [P, 1])
        mask = sb("mask", [P, BATCHES])
        u_odd = sb("u_odd", [LR, P])
        u_sb = sb("u_sb", [LR, P])
        uT = sb("uT", [STACK, P], F32R)
        stats = sb("stats2", [P, 2, 6])
        mean_var = sb("mean_var2", [P, 2])
        var_eps = sb("var_eps2", [P, 1])
        rstd = sb("rstd2", [P, 1])

        loaded = [sem(f"loaded{i}") for i in range(2)]
        stage_loaded = [sem(f"wf_stage_loaded{i}") for i in range(4)]
        small_loaded, gates_ready, bo_scaled = sem("small_loaded"), sem("gates_ready"), sem("bo_scaled")
        lb_zeroed, lb_loaded, lb_hi_ready, lb_lo_ready = (sem(n) for n in ("lb_zeroed", "lb_loaded", "lb_hi_ready", "lb_lo_ready"))
        batch_ready = sem("batch_ready")
        mask_steps, stack_set = sem("mask_steps"), sem("stack_set")
        weight_hi, weight_lo = sem("w_hi"), sem("w_lo")
        at_hi, at_lo, x_biased = sem("at_hi"), sem("at_lo"), sem("x_biased")
        o_done, x1_ready = sem("o_done"), sem("x1_ready")
        stats_ready, mean_ready, var_ready, rstd_ready, x2_ready = (
            sem(n) for n in ("stats_ready2", "mean_ready2", "var_ready2", "rstd_ready2", "x2_ready"))
        x2_turned, x2_hi, x2_full, x2_lo = sem("x2_turned"), sem("x2_hi"), sem("x2_full"), sem("x2_lo")
        u_done, u_odd_ready, u_ready, u_hi, u_lo = (
            sem(n) for n in ("u_done", "u_odd_ready", "u_ready", "u_hi", "u_lo"))
        f_done, out_ready = sem("f_done"), sem("out_ready")
        out_stored = [sem(f"out_stored{i}") for i in range(2)]

        stage_tiles = x1 + out_sb
        lb_stage = flat(x2T_full[:, :, :])

        loop_pairs = 14
        before = [Batch(a) for a in (-2, -1, 0)]
        after = [Batch(a) for a in range(2 * loop_pairs + 1, BATCHES)]

        def iterations(engine, body):
            for i in before[1:]:
                body(i)
            with engine.Fori(0, loop_pairs) as pair:
                body(Batch(1, pair))
                body(Batch(2, pair))
            for i in after:
                body(i)

        block = ctx.enter_context(nc.Block())

        @block.sync
        def _(sp):
            def load(b):
                if not b.exists():
                    return
                need(sp, at_lo, b.n - 1)
                need(sp, x1_ready, b.n * 2 - 2)
                sp.dma_start(at_raw[b.par][:, :], at_dram[b.n]).then_inc(loaded[b.par], DMA)
                sp.dma_start(x_in[b.par][:, :], x[b.n]).then_inc(loaded[b.par], DMA)

            def load_stage(w):
                if w >= 4:
                    sp.wait_ge(weight_lo, w - 3)
                sp.dma_start(stage_tiles[w % 4][:, :], w_t[w * P:(w + 1) * P, :]).then_inc(stage_loaded[w % 4], DMA)

            for dst, src in ((gates[:, 0:1], g_xattn), (gates[:, 1:2], g_ffn), (bo_row[:, :], bo),
                             (starts_i[:, :], starts)):
                sp.dma_start(dst, src.partition_broadcast(P)).then_inc(small_loaded, DMA)
            sp.dma_start(la[:, :, :], lora_a_t.rearrange("(k p) r -> p k r", p=P)).then_inc(small_loaded, DMA)
            load(Batch(0))
            for w in range(4):
                load_stage(w)
            sp.wait_ge(lb_zeroed, 1)
            sp.dma_start(lb_stage[0:LR, :], lora_b_t).then_inc(lb_loaded, DMA)
            sp.dma_start(lb_stage[LR:LR + 1, :], bias.unsqueeze(0)).then_inc(lb_loaded, DMA)
            sp.dma_start(lb_stage[LO_ROW:STACK, :], lora_b_t).then_inc(lb_loaded, DMA)
            for w in range(4, KC):
                load_stage(w)

            def body(i):
                load(i + 3)
                if i.exists():
                    need(sp, out_ready, i.n * 2 + 2)
                    sp.dma_start(out[i.n], out_sb[i.par][:, :]).then_inc(out_stored[i.par], DMA)

            body(before[0])
            iterations(sp, body)
            for i in range(2):
                sp.wait_ge(out_stored[i], DMA * (BATCHES // 2))

        @block.tensor
        def _(pe):
            def group(ps, b, g, act_t, w, extra):
                for r in range(GROUP_MM):
                    k, term = divmod(r, TERMS)
                    mm = nc.tensor.matmul(ps[:, :], act_t[term // 2][:, k, :],
                                          w[term % 2][:, k, g * HALF:(g + 1) * HALF],
                                          start=(r == 0), stop=(r == GROUP_MM - 1 and not extra))
                if extra:
                    need(pe, u_lo, b.n + 1)
                    cols = slice(g * HALF, (g + 1) * HALF)
                    nc.tensor.matmul(ps[:, :], uT[:, :], lb_hi[:, cols], start=False, stop=False)
                    mm = nc.tensor.matmul(ps[:, :], uT[0:LR + 1, :], lb_lo[:, cols], start=False, stop=True)
                return mm

            def out_projection(b, g):
                if not b.exists():
                    return
                need(pe, at_lo, b.n + 1)
                need(pe, x1_ready, b.n * 2 + g - 1)
                group(o_ps[g], b, g, atT[b.par], wos, False).then_inc(o_done, 1)

            def feed_forward(b, g):
                if not b.exists():
                    return
                if b.at(0) and g == 0:
                    pe.wait_ge(weight_lo, KC)
                    pe.wait_ge(lb_lo_ready, 1)
                need(pe, x2_lo, b.n * 2 + 2)
                need(pe, out_ready, b.n * 2 + g - 1)
                group(f_ps[g], b, g, x2T, wfs, True).then_inc(f_done, 1)

            def turn_x2(b):
                if not b.exists():
                    return
                need(pe, x2_ready, b.n + 1)
                for f in range(2):
                    need(pe, x2_lo, b.n * 2 + f - 1)
                    need(pe, x2_full, b.n * 2 + f - 1)
                    for i in range(4):
                        k = 4 * f + i
                        mm = nc.tensor.transpose(turn_ps[f][:, i * P:(i + 1) * P],
                                                 out_sb[b.par][:, k * P:(k + 1) * P], ident[:, :])
                    mm.then_inc(x2_turned, 1)

            def lora_down(b):
                if not b.exists():
                    return
                if b.at(0):
                    pe.wait_ge(small_loaded, 5 * DMA)
                need(pe, x2_full, b.n * 2 + 2)
                need(pe, u_ready, b.n)
                for k in range(KC):
                    row = LO_ROW * (k % 2)
                    mm = nc.tensor.matmul(u_ps[k % 2][row:row + LR, 0:P], la[:, k, :], x2T_full[:, k, :],
                                          start=(k < 2), stop=(k >= KC - 2))
                mm.then_inc(u_done, 1)

            def body(i):
                out_projection(i + 1, 0)
                lora_down(i)
                out_projection(i + 1, 1)
                feed_forward(i, 0)
                feed_forward(i, 1)
                turn_x2(i + 1)

            pe.wait_ge(shared.wo_lo, KC)
            body(before[0])
            iterations(pe, body)

        @block.scalar
        def _(act):
            act.wait_ge(small_loaded, 5 * DMA)
            nc.scalar.activation(tanhs[:, :], gates[:, :], ACT.Tanh).then_inc(gates_ready, 1)
            def high_at(b):
                if not b.exists():
                    return
                need(act, loaded[b.par], (b.earlier + 1) * 2 * DMA)
                need(act, o_done, b.n * 2 - 2)
                nc.scalar.activation(atT[b.par][0][:, :, :].rearrange("p k t -> p (k t)"), at_raw[b.par][:, :],
                                     ACT.Copy).then_inc(at_hi, 1)

            def high_x2(b):
                if not b.exists():
                    return
                if b.at(0):
                    act.wait_ge(lb_lo_ready, 1)
                need(act, f_done, b.n * 2)
                need(act, u_done, b.n)
                for f in range(2):
                    need(act, x2_turned, b.n * 2 + f + 1)
                    part = slice(4 * f, 4 * f + 4)
                    nc.scalar.activation(x2T[0][:, part, :].rearrange("p k t -> p (k t)"), turn_ps[f][:, :],
                                         ACT.Copy).then_inc(x2_hi, 1)
                    nc.scalar.activation(x2T_full[:, part, :].rearrange("p k t -> p (k t)"), turn_ps[f][:, :],
                                         ACT.Copy).then_inc(x2_full, 1)

            def body(i):
                high_at(i + 2)
                high_x2(i + 1)

            body(before[0])
            for w in range(KC):
                act.wait_ge(stage_loaded[w % 4], DMA * (w // 4 + 1))
                nc.scalar.activation(wfs[0][:, w, :], stage_tiles[w % 4][:, :], ACT.Copy).then_inc(weight_hi, 1)
                if w == 3:
                    act.wait_ge(lb_loaded, 3 * DMA)
                    nc.scalar.activation(lb_hi[:, :], lb_stage[0:STACK, :], ACT.Copy).then_inc(lb_hi_ready, 1)
            iterations(act, body)

        @block.vector
        def _(dve):
            nc.vector.memset(lb_stage, 0.0).then_inc(lb_zeroed, 1)
            dve.wait_ge(small_loaded, 5 * DMA)
            dve.wait_ge(batch_ready, 2)
            nc.vector.tensor_copy(starts_f[:, :], starts_i[:, :]).then_inc(mask_steps, 1)
            nc.vector.tensor_copy(batch_f[:, :], batch_i[:, :]).then_inc(mask_steps, 1)
            nc.vector.tensor_copy(row_f[:, :], row_i[:, :]).then_inc(mask_steps, 1)
            dve.wait_ge(mask_steps, 3)
            nc.vector.tensor_scalar(begun[:, :], batch_f[:, :], starts_f[:, 0:1], None, ALU.is_ge).then_inc(mask_steps, 1)
            for k in range(1, ADAPTERS + 1):
                dve.wait_ge(mask_steps, 3 + k)
                nc.vector.scalar_tensor_tensor(out=begun[:, :], in0=batch_f[:, :], scalar=starts_f[:, k:k + 1],
                                               in1=begun[:, :], op0=ALU.is_ge, op1=ALU.add).then_inc(mask_steps, 1)
            dve.wait_ge(mask_steps, 4 + ADAPTERS)
            nc.vector.tensor_scalar(uT[LO_ROW // 2:LO_ROW, :],
                                    row_f[LO_ROW // 2:LO_ROW, 0:1].broadcast_to([LO_ROW // 2, P]), float(LR), None,
                                    ALU.is_equal).then_inc(stack_set, 1)
            dve.wait_ge(stack_set, 1)
            nc.vector.tensor_scalar(begun_at[:, :], row_f[:, :], float(RANK), 2.0, ALU.is_ge, ALU.add).then_inc(mask_steps, 1)
            steps = 5 + ADAPTERS
            for at_row, by in ((2 * RANK, 1.0), (LO_ROW, -2.0), (LO_ROW + RANK, 1.0), (LO_ROW + 2 * RANK, 1.0)):
                dve.wait_ge(mask_steps, steps)
                nc.vector.tensor_scalar(row_step[:, :], row_f[:, :], float(at_row), by, ALU.is_ge,
                                        ALU.mult).then_inc(mask_steps, 1)
                dve.wait_ge(mask_steps, steps + 1)
                nc.vector.tensor_tensor(begun_at[:, :], begun_at[:, :], row_step[:, :], ALU.add).then_inc(mask_steps, 1)
                steps += 2
            dve.wait_ge(mask_steps, steps)
            nc.vector.tensor_scalar(mask[:, :], begun[:, :], float(ADAPTERS + 1), begun_at[:, 0:1], ALU.min,
                                    ALU.is_equal).then_inc(mask_steps, 1)
            dve.wait_ge(gates_ready, 1)
            nc.vector.tensor_scalar(bo_row[:, :], bo_row[:, :], tanhs[:, 0:1], None, ALU.mult).then_inc(bo_scaled, 1)
            for w in range(KC):
                dve.wait_ge(weight_hi, w + 1)
                nc.vector.tensor_tensor(wfs[1][:, w, :], stage_tiles[w % 4][:, :], wfs[0][:, w, :],
                                        ALU.subtract).then_inc(weight_lo, 1)
                if w == 4:
                    dve.wait_ge(lb_hi_ready, 1)
                    nc.vector.tensor_tensor(lb_lo[:, :], lb_stage[0:LR + 1, :], lb_hi[0:LR + 1, :],
                                            ALU.subtract).then_inc(lb_lo_ready, 1)
            dve.wait_ge(mask_steps, steps + 1)
            dve.wait_ge(weight_lo, KC)

            def attended(b, g):
                if not b.exists():
                    return
                cols = slice(g * HALF, (g + 1) * HALF)
                need(dve, o_done, b.n * 2 + g + 1)
                need(dve, x_biased, b.n + 1)
                need(dve, out_ready, b.n * 2 - 2)
                nc.vector.scalar_tensor_tensor(out=x1[b.par][:, cols], in0=o_ps[g][:, :], scalar=tanhs[:, 0:1],
                                               in1=x_in[b.par][:, cols], op0=ALU.mult,
                                               op1=ALU.add).then_inc(x1_ready, 1)

            def norm(b):
                if not b.exists():
                    return
                for h in range(2):
                    need(dve, x1_ready, b.n * 2 + h + 1)
                    nc.vector.bn_stats(stats[:, h, :], x1[b.par][:, h * HALF:(h + 1) * HALF]).then_inc(stats_ready, 1)
                dve.wait_ge(mask_steps, 3)
                need(dve, stats_ready, b.n * 2 + 2)
                nc.vector.bn_aggr(mean_var[:, :], stats[:, :, :].rearrange("p h s -> p (h s)")).then_inc(mean_ready, 1)
                need(dve, mean_ready, b.n + 1)
                nc.vector.tensor_scalar(var_eps[:, :], mean_var[:, 1:2], EPS, None, ALU.add).then_inc(var_ready, 1)
                need(dve, rstd_ready, b.n + 1)
                need(dve, out_stored[b.par], b.earlier * DMA)
                nc.vector.tensor_scalar(out_sb[b.par][:, :], x1[b.par][:, :], mean_var[:, 0:1], rstd[:, 0:1],
                                        ALU.subtract, ALU.mult).then_inc(x2_ready, 1)

            def outputs(b, g):
                if not b.exists():
                    return
                cols = slice(g * HALF, (g + 1) * HALF)
                need(dve, f_done, b.n * 2 + g + 1)
                nc.vector.scalar_tensor_tensor(out=out_sb[b.par][:, cols], in0=f_ps[g][:, :], scalar=tanhs[:, 1:2],
                                               in1=x1[b.par][:, cols], op0=ALU.mult,
                                               op1=ALU.add).then_inc(out_ready, 1)

            def low_x2(b):
                if not b.exists():
                    return
                for f in range(2):
                    need(dve, x2_full, b.n * 2 + f + 1)
                    hi, lo = (t[:, 4 * f:4 * f + 4, :].rearrange("p k t -> p (k t)") for t in x2T)
                    nc.vector.tensor_tensor(lo, turn_ps[f][:, :], hi, ALU.subtract).then_inc(x2_lo, 1)

            def split_u(b):
                if not b.exists():
                    return
                need(dve, u_done, b.n + 1)
                nc.vector.tensor_scalar(u_odd[:, :], u_ps[1][LO_ROW:STACK, 0:P], mask[LO_ROW:STACK, bass.ds(b.n, 1)], None,
                                        ALU.mult).then_inc(u_odd_ready, 1)
                need(dve, u_odd_ready, b.n + 1)
                nc.vector.scalar_tensor_tensor(out=u_sb[:, :], in0=u_ps[0][0:LR, 0:P], scalar=mask[0:LR, bass.ds(b.n, 1)],
                                               in1=u_odd[:, :], op0=ALU.mult, op1=ALU.add).then_inc(u_ready, 1)
                need(dve, u_ready, b.n + 1)
                need(dve, f_done, b.n * 2)
                nc.vector.tensor_copy(uT[0:LR, :], u_sb[:, :]).then_inc(u_hi, 1)
                need(dve, u_hi, b.n + 1)
                nc.vector.tensor_tensor(uT[LO_ROW:STACK, :], u_sb[:, :], uT[0:LR, :], ALU.subtract).then_inc(u_lo, 1)

            def body(i):
                attended(i + 1, 0)
                split_u(i)
                attended(i + 1, 1)
                norm(i + 1)
                outputs(i, 0)
                outputs(i, 1)
                low_x2(i + 1)

            body(before[0])
            iterations(dve, body)

        @block.gpsimd
        def _(pool):
            nc.gpsimd.iota(batch_i[:, :], pattern=[[1, BATCHES]], base=0, channel_multiplier=0).then_inc(batch_ready, 1)
            nc.gpsimd.iota(row_i[:, :], pattern=[[0, 1]], base=0, channel_multiplier=1).then_inc(batch_ready, 1)
            pool.wait_ge(bo_scaled, 1)

            def low_at_and_bias(b):
                if not b.exists():
                    return
                need(pool, at_hi, b.n + 1)
                hi, lo = (t[:, :, :].rearrange("p k t -> p (k t)") for t in atT[b.par])
                nc.gpsimd.tensor_tensor(lo, at_raw[b.par][:, :], hi, ALU.subtract).then_inc(at_lo, 1)
                nc.gpsimd.tensor_tensor(x_in[b.par][:, :], x_in[b.par][:, :], bo_row[:, :],
                                        ALU.add).then_inc(x_biased, 1)

            def inverse_std(b):
                if not b.exists():
                    return
                need(pool, var_ready, b.n + 1)
                nc.gpsimd.tensor_tensor(rstd[:, :], var_eps[:, :], minus_half[:, :], ALU.pow).then_inc(rstd_ready, 1)

            def body(i):
                low_at_and_bias(i + 2)
                inverse_std(i + 1)

            body(before[0])
            iterations(pool, body)


def build_program(nc, x, ctx_in, g_xattn, g_ffn, wq, bq, wk, bk, wv, bv, wo, bo, w_t, bias, lora_a_t, lora_b_t,
                  starts, out):
    at_dram = nc.dram_tensor("attention_out", (BATCHES, P, EMBED), F32).ap()
    with ExitStack() as ctx:
        shared = Shared(nc, ctx)
        attention_phase(nc, shared, x, ctx_in, wq, bq, wk, bk, wv, bv, wo, at_dram)
        ffn_phase(nc, shared, x, g_xattn, g_ffn, bo, w_t, bias, lora_a_t, lora_b_t, starts, at_dram, out)


def kernel(x, ctx_4096, g_xattn, g_ffn, L0_xattn_Wq, L0_xattn_bq, L0_xattn_Wk, L0_xattn_bk, L0_xattn_Wv,
           L0_xattn_bv, L0_xattn_Wo, L0_xattn_bo, L0_ffn_weight, L0_ffn_bias, L0_ffn_lora_A, L0_ffn_lora_B,
           L0_ffn_lora_start_indices):
    import numpy as np
    import concourse.bacc as bacc
    from concourse.bass_utils import run_bass_kernel_spmd

    nc = bacc.Bacc("TRN2", target_bir_lowering=False, num_devices=1)
    lora_b = np.asarray(L0_ffn_lora_B)
    ins = {
        "x": x, "ctx": ctx_4096, "g_xattn": g_xattn, "g_ffn": g_ffn,
        "wq": L0_xattn_Wq, "bq": L0_xattn_bq, "wk": L0_xattn_Wk, "bk": L0_xattn_bk,
        "wv": L0_xattn_Wv, "bv": L0_xattn_bv, "wo": L0_xattn_Wo, "bo": L0_xattn_bo,
        "w_t": np.asarray(L0_ffn_weight).T, "bias": L0_ffn_bias,
        "lora_a_t": np.asarray(L0_ffn_lora_A).reshape(-1, EMBED).T,
        "lora_b_t": lora_b.transpose(0, 2, 1).reshape(-1, EMBED),
        "starts": L0_ffn_lora_start_indices,
    }
    arrays, args = {}, []
    for name, a in ins.items():
        a = np.ascontiguousarray(a)
        arrays[f"in_{name}"] = a
        args.append(nc.dram_tensor(f"in_{name}", a.shape, mybir.dt.from_np(a.dtype), kind="ExternalInput").ap())
    args.append(nc.dram_tensor("out_x", (BATCHES, P, EMBED), F32, kind="ExternalOutput").ap())
    build_program(nc, *args)
    r = run_bass_kernel_spmd(nc, [arrays], core_ids=[0])
    return r.results[0]["out_x"]
```

```python
from contextlib import ExitStack

import concourse.bass as bass
from concourse import mybir

F32 = mybir.dt.float32
F32R = mybir.dt.float32r
I32 = mybir.dt.int32
ALU = mybir.AluOpType
ACT = mybir.ActivationFunctionType
AX_X = mybir.AxisListType.X

P = 128
BATCHES = 32
EMBED = 1024
KC = EMBED // P
NUM_KV = 8
GROUPS = 4
DH = 32
KVD = NUM_KV * DH
HALF = EMBED // 2
UNITS = 8
SCALE = float(DH) ** -0.5
EPS = 1e-5
ADAPTERS = 3
RANK = 16
LR = ADAPTERS * RANK
LO_ROW = 64
STACK = LO_ROW + LR
DMA = 16
TERMS = 3
GROUP_MM = KC * TERMS


class Batch:

    def __init__(self, offset, pair=0):
        self.n = pair * 2 + offset if not isinstance(pair, int) else 2 * pair + offset
        self.par = offset % 2
        self.earlier = pair + offset // 2
        self.pair, self.offset = pair, offset

    def __add__(self, k):
        return Batch(self.offset + k, self.pair)

    def exists(self):
        return not isinstance(self.n, int) or 0 <= self.n < BATCHES

    def at(self, n):
        return isinstance(self.n, int) and self.n == n


def need(engine, semaphore, count):
    if not isinstance(count, int) or count > 0:
        engine.wait_ge(semaphore, count)


def unit_of(a, s):
    return (a, s) if s >= 0 else (a + (-1), s + UNITS)


def flat(t):
    return t.rearrange("p a b -> p (a b)") if len(t.shape) == 3 else t.rearrange("p a b c -> p (a b c)")


class Shared:

    def __init__(self, nc, ctx, x, at_dram):
        def sb(name, shape, dt=F32):
            return ctx.enter_context(nc.sbuf_tensor(name, shape, dt))

        def sem(name):
            return ctx.enter_context(nc.semaphore(name))

        self.nc, self.x, self.at_dram = nc, x, at_dram
        self.wkv = [sb(f"wkv_{t}", [P, KC, 2 * KVD], F32R) for t in ("hi", "lo")]
        self.wide = [sb(f"wide_{t}", [P, KC, EMBED], F32R) for t in ("hi", "lo")]
        self.wos = [self.wkv, [t[:, :, 0:HALF] for t in self.wide]]
        self.raw_c = [sb(f"raw_c{i}", [P, EMBED]) for i in range(2)]
        self.raw_x = [sb(f"raw_x{i}", [P, EMBED]) for i in range(2)]
        self.ctxT = [sb(f"ctxT_{t}", [P, KC, P], F32R) for t in ("hi", "lo")]
        self.xT = [sb(f"xT_{t}", [P, KC, P], F32R) for t in ("hi", "lo")]
        self.atT = [self.ctxT, self.xT]
        self.result = [sb(f"result{i}", [P, EMBED]) for i in range(2)]
        self.bo_row = sb("bo_row", [P, EMBED])
        self.gates = sb("gates", [P, 2])
        self.tanhs = sb("tanhs", [P, 2])
        self.mask = sb("mask", [P, BATCHES])
        self.row_f = sb("row_f", [P, 1])
        self.ident = sb("ident", [P, P])
        self.minus_half = sb("minus_half", [P, 1])
        self.bank = [ctx.enter_context(nc.psum_tensor(f"bank{i}", [P, HALF], F32)) for i in range(8)]
        self.o_ps = self.bank[0:2]
        self.at_stored = [sem(f"at_stored{i}") for i in range(2)]
        self.gates_loaded, self.gates_ready, self.bo_scaled = sem("gates_loaded"), sem("gates_ready"), sem("bo_scaled")
        self.wo_loaded = [sem(f"wo_loaded{i}") for i in range(4)]
        self.wo_hi = sem("wo_hi")
        self.wo_lo = sem("wo_lo")
        self.at_loaded = [sem(f"at_loaded{i}") for i in range(2)]
        self.x_in_loaded = [sem(f"x_in_loaded{i}") for i in range(2)]
        self.at_hi, self.at_lo, self.x_biased = sem("at_hi"), sem("at_lo"), sem("x_biased")
        self.o_done, self.x1_ready = sem("o_done"), sem("x1_ready")

    def wo_stage(self, w):
        return (self.raw_c + self.raw_x)[w % 4]

    def wo_part(self, w, t):
        k = 2 * (w % 4)
        return self.wos[w // 4][t][:, k:k + 2, :]

    def load_at(self, sp, b):
        need(sp, self.at_lo, b.n - 1)
        need(sp, self.at_stored[b.par], (b.earlier + 1) * DMA)
        sp.dma_start(self.raw_c[b.par][:, :], self.at_dram[b.n]).then_inc(self.at_loaded[b.par], DMA)

    def load_x_in(self, sp, b):
        need(sp, self.x1_ready, b.n * 2 - 2)
        sp.dma_start(self.raw_x[b.par][:, :], self.x[b.n]).then_inc(self.x_in_loaded[b.par], DMA)

    def high_at(self, act, b):
        need(act, self.at_loaded[b.par], (b.earlier + 1) * DMA)
        need(act, self.o_done, b.n * 2 - 2)
        self.nc.scalar.activation(flat(self.atT[b.par][0][:, :, :]), self.raw_c[b.par][:, :],
                                  ACT.Copy).then_inc(self.at_hi, 1)

    def low_at(self, engine, ops, b):
        need(engine, self.at_hi, b.n + 1)
        hi, lo = (flat(t[:, :, :]) for t in self.atT[b.par])
        ops.tensor_tensor(lo, self.raw_c[b.par][:, :], hi, ALU.subtract).then_inc(self.at_lo, 1)

    def bias_x(self, pool, b):
        need(pool, self.x_in_loaded[b.par], (b.earlier + 1) * DMA)
        t = self.raw_x[b.par][:, :]
        self.nc.gpsimd.tensor_tensor(t, t, self.bo_row[:, :], ALU.add).then_inc(self.x_biased, 1)

    def out_matmul(self, b, g, r):
        k, term = divmod(r, TERMS)
        return self.nc.tensor.matmul(self.o_ps[g][:, :], self.atT[b.par][term // 2][:, k, :],
                                     self.wos[g][term % 2][:, k, :], start=(r == 0), stop=(r == GROUP_MM - 1))


def attention_phase(nc, shared, x, x_t, ctx_in, g_xattn, g_ffn, wq, bq, wk, bk, wv, bv, wo, bo, starts, at_dram):
    with ExitStack() as ctx:
        def sb(name, shape, dt=F32):
            return ctx.enter_context(nc.sbuf_tensor(name, shape, dt))

        def sem(name):
            return ctx.enter_context(nc.semaphore(name))

        bank = shared.bank
        mm_ps, score_ps, at_ps, turn_ps = bank[0:2], bank[2:4], bank[4], bank[5:8]

        wkv, wqs, ctxT, xT = shared.wkv, shared.wide, shared.ctxT, shared.xT
        c_raw, xt_raw, ident, minus_half = shared.raw_c, shared.raw_x, shared.ident, shared.minus_half
        x_nat = sb("x_nat", [P, EMBED])
        moments = [sb(f"moments{i}", [P, P, 2]) for i in range(2)]
        moments_dram = nc.dram_tensor("moments", (BATCHES, P, 2), F32).ap()
        q_sb = sb("q_sb", [P, 2, GROUPS, 4 * DH])
        q_halves = sb("q_halves", [P, 2, GROUPS * 4, 2, DH], F32R)
        qT = sb("qT", [P, 2, GROUPS * 2, P], F32R)
        k_twice = [sb(f"k_twice_{t}", [P, NUM_KV, 2, DH], F32R) for t in ("hi", "lo")]
        kD = [[sb(f"kD{i}_{t}", [P, NUM_KV // 2, 2, P], F32R) for t in ("hi", "lo")] for i in range(2)]
        k_sb = sb("k_sb", [P, KVD])
        values = [sb(f"values{i}", [P, KVD]) for i in range(2)]
        probs_all = sb("probs_all", [P, 4, 4, P])
        probs = [probs_all[:, i] for i in range(4)]
        probsT = [sb(f"probsT{i}", [P, 4, P]) for i in range(2)]
        at_sb = shared.result
        ident_r = sb("ident_r", [P, P], F32R)
        bq_row = shared.bo_row
        bkv_row = sb("bkv_row", [P, 2 * KVD])
        row_max = sb("row_max", [P, UNITS, 4])
        neg_max = sb("neg_max", [P, UNITS, 4])
        row_sum = sb("row_sum", [P, UNITS, 4])
        inv_sum = sb("inv_sum", [P, UNITS, 4])
        starts_i = sb("starts_i", [P, ADAPTERS + 1], I32)
        starts_f = sb("starts_f", [P, ADAPTERS + 1])
        batch_i = sb("batch_i", [P, BATCHES], I32)
        batch_f = sb("batch_f", [P, BATCHES])
        begun = sb("begun", [P, BATCHES])
        row_i = sb("row_i", [P, 1], I32)
        row_step = sb("row_step", [P, 1])
        begun_at = sb("begun_at", [P, 1])
        stats = sb("stats", [P, 2, 6])
        mean_var = sb("mean_var", [P, 2])
        var_eps = sb("var_eps", [P, 1])

        c_loaded = [sem(f"c_loaded{i}") for i in range(2)]
        x_loaded = sem("x_loaded")
        xt_loaded = [sem(f"xt_loaded{i}") for i in range(2)]
        moments_stored, bo_loaded = sem("moments_stored"), sem("bo_loaded")
        moments_loaded = [sem(f"moments_loaded{i}") for i in range(2)]
        stage_loaded = [sem(f"stage_loaded{i}") for i in range(4)]
        starts_loaded, batch_ready, mask_steps = sem("starts_loaded"), sem("batch_ready"), sem("mask_steps")
        biases_loaded, bq_loaded = sem("biases_loaded"), sem("bq_loaded")
        at_stored = shared.at_stored
        ident_zeroed, ident_ready, ident_r_ready = sem("ident_zeroed"), sem("ident_ready"), sem("ident_r_ready")
        kd_zeroed = sem("kd_zeroed")
        weight_hi, weight_lo = sem("weight_hi"), sem("weight_lo")
        turned = {k: sem(f"{k}_turned") for k in "qk"}
        hi_ready = {k: sem(f"{k}T_hi") for k in "cx"}
        lo_ready = {k: sem(f"{k}T_lo") for k in "cx"}
        qT_by_act, qT_by_dve = sem("qT_by_act"), sem("qT_by_dve")
        kD_by_act, kD_by_dve = sem("kD_by_act"), sem("kD_by_dve")
        q_hi_ready, q_lo_ready, k_hi_ready, k_lo_ready = (
            sem(n) for n in ("q_hi_ready", "q_lo_ready", "k_hi_ready", "k_lo_ready"))
        projected, drained, keys_drained = sem("projected"), sem("drained"), sem("keys_drained")
        stats_ready, mean_ready, var_ready = sem("stats_ready"), sem("mean_ready"), sem("var_ready")
        rstd_ready, x_centred, xn_ready = sem("rstd_ready"), sem("x_centred"), sem("xn_ready")
        scored, row_max_ready, neg_max_ready = sem("scored"), sem("row_max_ready"), sem("neg_max_ready")
        exp_done, inv_ready, probs_ready = sem("exp_done"), sem("inv_ready"), sem("probs_ready")
        probs_turned = sem("probs_turned")
        probsT_ready = [sem("probsT_by_act"), sem("probsT_by_dve")]
        values_summed, at_ready = sem("values_summed"), sem("at_ready")

        PARTS = {"c": 2, "x": 2, "q": 4, "k": 2}

        def count(kind, b, part):
            return b.n * PARTS[kind] + part + 1

        def context_slots(a, lows):
            return (0, 2) if a.at(-2) else (4, 5) if lows else (1, 4)

        X_SLOTS = (6, 7)
        CENTRE_SLOT, SCALE_SLOT = 0, 4

        def centre_slot(a):
            return SCALE_SLOT if a.at(-2) else 3 if a.at(-1) or a.at(0) else CENTRE_SLOT

        def stats_slot(a):
            return 6 if a.at(-2) else 5 if a.at(-1) else 2

        def raw_part(part):
            return slice(part * HALF, (part + 1) * HALF)

        def left_bank(kind, b, part):
            if kind == "q":
                return (qT_by_act, qT_by_dve)[part % 2], b.n * 2 + part // 2 + 1
            if kind == "p":
                return probsT_ready[part % 2], b.n * 4 + part // 2 + 1
            return (kD_by_act, kD_by_dve)[part], b.n + 1

        def fills(a):
            return [(None, None), (None, ("q", a, 2)), (None, ("q", a, 3)), (("k", a + 1, 0), None),
                    (None, ("k", a + 1, 1)), (None, ("q", a + 1, 0)),
                    (("q", a + 1, 1), None), (None, None)]

        def fill_in(a, s, late):
            if s < 0:
                a, s = a + (-1), s + UNITS
            f = fills(a)[s][late]
            return f if f is not None and f[1].exists() else None

        PLACES = [(s, step) for s in range(UNITS) for step in range(3) if step or s in (3, 6)]

        def turn_bank(s, step):
            return turn_ps[PLACES.index((s % UNITS, step)) % len(turn_ps)]

        def bank_before(a, s, step):
            place = PLACES.index((s, step)) - len(turn_ps)
            for _ in range(2 * len(PLACES)):
                it, at = (a, place) if place >= 0 else (a + (-1), place + len(PLACES))
                if at < 0:
                    return None
                s, step = PLACES[at]
                if step == 1:
                    b, unit = unit_of(it, s - 2)
                    f = ("p", b, unit)
                else:
                    f = fills(it)[s][step // 2]
                if f is not None and f[1].exists():
                    return f
                place -= len(turn_ps)
            return None

        def group_of(a, m):
            i, r = divmod(m, GROUP_MM)
            return (a + 1, i + 1, r) if i < 2 else (a + 2, 0, r)

        def mm_bank(b, g):
            return mm_ps[(b.par + g) % 2]

        KV_STAGES = KC // 2
        STAGES = 3 * KV_STAGES
        SPLITS = {(-2, 0): [0], (-2, 1): [1], (-2, 2): [2], (-2, 3): [3], (-2, 5): [4], (-2, 6): [5],
                  (-2, 7): [6], (-1, 0): [7, 8], (-1, 1): [9], (-1, 2): [10, 11]}
        stage_tiles = [at_sb[0][:, :], at_sb[1][:, :]] + [
            probs_all[:, 2 * i:2 * i + 2].rearrange("p u q k -> p (u q k)") for i in range(2)]

        def stage_count(w):
            return 2 * DMA + DMA * (w // 4)

        def stage_parts(w):
            k = 2 * (w % KV_STAGES)
            g = w // KV_STAGES
            hi, lo = (t[:, k:k + 2, :] if g == 0 else t[:, k:k + 2, (g - 1) * HALF:g * HALF]
                      for t in (wqs if g else wkv))
            return stage_tiles[w % 4].rearrange("p (k n) -> p k n", k=2), hi, lo

        def stages_in(a, s):
            return SPLITS.get((a.n, s), []) if isinstance(a.n, int) else []

        def twice(keys):
            return keys[:, :].rearrange("p (g d) -> p g d", d=DH).unsqueeze(2).broadcast_to(
                [P, NUM_KV, 2, DH])

        loop_pairs = 14
        before = [Batch(a) for a in (-2, -1, 0)]
        after = [Batch(a) for a in range(2 * loop_pairs + 1, BATCHES + 1)]

        def late_slot(a, s):
            return (a.n - 30) * UNITS + s if isinstance(a.n, int) and a.n >= 30 else None

        WO_HI, AT_HI, AT_LO, BIAS_X = (1, 3, 5, 6, 7, 8, 9, 10), (11, 12), (12, 13), (14, 15)
        BO_SLOT = BIAS_X[0] - 1
        OUT_MM, MM_PER_SLOT = 13, 9

        def split_in(a, s, behind):
            t = late_slot(a, s)
            return WO_HI.index(t - behind) if t is not None and t - behind in WO_HI else None

        def iterations(engine, body, first=before[1:]):
            for a in first:
                body(a)
            with engine.Fori(0, loop_pairs) as pair:
                body(Batch(1, pair))
                body(Batch(2, pair))
            for a in after:
                body(a)

        block = ctx.enter_context(nc.Block())

        @block.sync
        def _(sp):
            wk_v = wk.rearrange("(k p) n -> p k n", p=P)
            wq_v = wq.rearrange("(k p) n -> p k n", p=P)
            wv_v = wv.rearrange("(k p) n -> p k n", p=P)
            wo_v = wo.rearrange("(k p) n -> p k n", p=P)

            def load_c(b):
                if b.exists():
                    need(sp, lo_ready["c"], (b + (-2)).n * 2 + 2)
                    sp.dma_start(c_raw[b.par][:, :], ctx_in[b.n]).then_inc(c_loaded[b.par], DMA)

            def load_xt(b):
                if b.exists():
                    need(sp, lo_ready["x"], (b + (-2)).n * 2 + 2)
                    sp.dma_start(xt_raw[b.par][:, :], x_t[b.n]).then_inc(xt_loaded[b.par], DMA)

            def load_x(b):
                if b.exists():
                    need(sp, stats_ready, b.n * 2)
                    sp.dma_start(x_nat[:, :], x[b.n]).then_inc(x_loaded, DMA)

            def store_moments(b):
                if b.exists():
                    need(sp, rstd_ready, b.n + 1)
                    sp.dma_start(moments_dram[b.n], mean_var[:, :]).then_inc(moments_stored, DMA)

            def spread_moments(b):
                if b.exists():
                    need(sp, moments_stored, (b.n + 1) * DMA)
                    sp.dma_start(moments[b.par][:, :, :],
                                 moments_dram[b.n].partition_broadcast(P)).then_inc(moments_loaded[b.par], DMA)

            def load_stage(w):
                if w >= 4:
                    sp.wait_ge(weight_lo, w - 3)
                tile = stage_tiles[w % 4]
                if w < KV_STAGES:
                    t = tile.rearrange("p (k n) -> p k n", k=2)
                    sp.dma_start(t[:, :, 0:KVD], wk_v[:, 2 * w:2 * w + 2, :]).then_inc(stage_loaded[w % 4], DMA)
                    sp.dma_start(t[:, :, KVD:], wv_v[:, 2 * w:2 * w + 2, :]).then_inc(stage_loaded[w % 4], DMA)
                else:
                    g, k = w // KV_STAGES - 1, 2 * (w % KV_STAGES)
                    sp.dma_start(tile.rearrange("p (k n) -> p k n", k=2),
                                 wq_v[:, k:k + 2, g * HALF:(g + 1) * HALF]).then_inc(stage_loaded[w % 4], DMA)

            def load_wo(w):
                k, cols = 2 * (w % 4), slice(w // 4 * HALF, (w // 4 + 1) * HALF)
                if w >= 4:
                    sp.wait_ge(shared.wo_lo, w - 3)
                sp.dma_start(shared.wo_stage(w)[:, :].rearrange("p (k n) -> p k n", k=2),
                             wo_v[:, k:k + 2, cols]).then_inc(shared.wo_loaded[w % 4], DMA)

            sp.dma_start(starts_i[:, :], starts.partition_broadcast(P)).then_inc(starts_loaded, DMA)
            load_c(Batch(0))
            load_x(Batch(0))
            for w in range(KV_STAGES):
                load_stage(w)
            load_xt(Batch(0))
            store_moments(Batch(0))
            sp.dma_start(bkv_row[:, 0:KVD], bk.partition_broadcast(P)).then_inc(biases_loaded, DMA)
            sp.dma_start(bkv_row[:, KVD:], bv.partition_broadcast(P)).then_inc(biases_loaded, DMA)
            load_stage(4)
            spread_moments(Batch(0))
            load_stage(5)
            load_x(Batch(1))
            load_stage(6)
            load_stage(7)
            load_c(Batch(1))
            load_stage(8)
            load_stage(9)
            sp.dma_start(bq_row[:, :], bq.partition_broadcast(P)).then_inc(bq_loaded, DMA)
            load_stage(10)
            load_xt(Batch(1))
            store_moments(Batch(1))
            load_stage(11)
            spread_moments(Batch(1))
            for dst, src in ((shared.gates[:, 0:1], g_xattn), (shared.gates[:, 1:2], g_ffn)):
                sp.dma_start(dst, src.partition_broadcast(P)).then_inc(shared.gates_loaded, DMA)

            def body(a):
                load_xt(a + 3)
                load_c(a + 3)
                load_x(a + 3)
                if a.at(30):
                    sp.wait_ge(lo_ready["c"], BATCHES * 2)
                    sp.wait_ge(lo_ready["x"], BATCHES * 2)
                    for w in range(4):
                        load_wo(w)
                if a.at(31):
                    sp.wait_ge(drained, 3 * BATCHES)
                    sp.dma_start(shared.bo_row[:, :], bo.partition_broadcast(P)).then_inc(bo_loaded, DMA)
                    for i in range(2):
                        sp.wait_ge(shared.wo_lo, 5 + i)
                        shared.load_at(sp, Batch(i))
                    for i in range(2):
                        sp.wait_ge(shared.wo_lo, 7 + i)
                        shared.load_x_in(sp, Batch(i))
                b = a + (-1)
                if b.exists():
                    need(sp, at_ready, b.n * 2 + 2)
                    sp.dma_start(at_dram[b.n], at_sb[b.par][:, :]).then_inc(at_stored[b.par], DMA)
                if a.at(30):
                    for w in range(4, KC):
                        load_wo(w)
                store_moments(a + 3)
                spread_moments(a + 3)

            iterations(sp, body)

        @block.tensor
        def _(pe):
            def bank_left(a, s, step):
                last = bank_before(a, s, step)
                if last is not None:
                    need(pe, *left_bank(*last))

            def transposes(a, s, late):
                f = fill_in(a, s, late)
                if f is None:
                    return
                kind, b, part = f
                bank_left(a, s, 2 * late)
                if kind == "q":
                    half, c0 = part // 2, part % 2 * 4
                    need(pe, q_lo_ready, b.n * 2 + half + 1)
                    src = [q_halves[:, half, 2 * c:2 * c + 2].rearrange("p q t d -> p (q t d)")
                           for c in range(c0, c0 + 4)]
                else:
                    need(pe, (k_hi_ready, k_lo_ready)[part], b.n + 1)
                    src = [k_twice[part][:, 2 * c:2 * c + 2].rearrange("p q t d -> p (q t d)") for c in range(4)]
                for i, t in enumerate(src):
                    dst = turn_bank(s, 2 * late)[:, i * P:(i + 1) * P]
                    mm = nc.tensor.transpose(dst.bitcast(F32R), t, ident_r[:, :])
                mm.then_inc(turned[kind], 1)

            def project(a, first, n):
                for m in range(first, first + n):
                    b, g, r = group_of(a, m)
                    if not b.exists():
                        continue
                    k, term = divmod(r, TERMS)
                    if r in (0, GROUP_MM // 2) and g < 2:
                        src = "x" if g else "c"
                        need(pe, lo_ready[src], count(src, b, int(r > 0)))
                    if r == 0:
                        need(pe, drained, b.n * 3 + g - 1)
                    if b.at(0) and r % (2 * TERMS) == 0:
                        pe.wait_ge(weight_lo, g * KV_STAGES + r // (2 * TERMS) + 1)
                    act_t = (xT if g else ctxT)[term // 2]
                    rhs = wqs[term % 2][:, k, (g - 1) * HALF:g * HALF] if g else wkv[term % 2][:, k, :]
                    mm = nc.tensor.matmul(mm_bank(b, g)[:, :], act_t[:, k, :], rhs,
                                          start=(r == 0), stop=(r == GROUP_MM - 1))
                    if r == GROUP_MM - 1:
                        mm.then_inc(projected, 1)

            def scores(b, s):
                if not b.exists():
                    return
                half, j = divmod(s, GROUPS)
                if j % 2 == 0:
                    need(pe, *left_bank("q", b, 2 * half + j // 2))
                if s == 0:
                    for part in range(2):
                        need(pe, *left_bank("k", b, part))
                need(pe, exp_done, b.n * UNITS + s - 1)
                for pair in range(2):
                    for t in range(2):
                        mm = nc.tensor.matmul(
                            score_ps[s % 2][:, pair * 2 * P:(pair + 1) * 2 * P], qT[:, half, 2 * j + pair, :],
                            kD[b.par][t][:, 2 * half + pair].rearrange("p q k -> p (q k)"),
                            start=(t == 0), stop=(t == 1))
                mm.then_inc(scored, 1)

            def turn_probs(a, slot):
                b, s = unit_of(a, slot - 2)
                if not b.exists():
                    return
                need(pe, probs_ready, b.n * UNITS + s + 1)
                bank_left(a, slot, 1)
                for q in range(4):
                    mm = nc.tensor.transpose(turn_bank(slot, 1)[:, q * P:(q + 1) * P], probs[s % 4][:, q, :],
                                             ident[:, :])
                mm.then_inc(probs_turned, 1)

            def sum_values(b, s):
                if not b.exists():
                    return
                half, j = divmod(s, GROUPS)
                if j == 0:
                    need(pe, at_ready, b.n * 2 + half)
                need(pe, probsT_ready[s % 2], b.n * 4 + s // 2 + 1)
                for q in range(4):
                    v0 = (4 * half + q) * DH
                    mm = nc.tensor.matmul(at_ps[q * DH:(q + 1) * DH, j * P:(j + 1) * P],
                                          values[b.par][:, v0:v0 + DH], probsT[s % 2][:, q, :],
                                          start=True, stop=True)
                mm.then_inc(values_summed, 1)

            def first_out_projection(a, s):
                t = late_slot(a, s)
                if t is None or t < OUT_MM:
                    return
                first = (t - OUT_MM) * MM_PER_SLOT
                for m in range(first, min(first + MM_PER_SLOT, 2 * GROUP_MM)):
                    g, r = divmod(m, GROUP_MM)
                    if r == 0:
                        pe.wait_ge(shared.wo_lo, 4 * g + 4)
                    if m == 0:
                        pe.wait_ge(shared.at_lo, 1)
                        pe.wait_ge(drained, 3 * BATCHES)
                    mm = shared.out_matmul(Batch(0), g, r)
                    if r == GROUP_MM - 1:
                        mm.then_inc(shared.o_done, 1)

            def body(a):
                for s in range(UNITS):
                    scores(a, s)
                    if s % 2 == 0:
                        sum_values(*unit_of(a, s - 4))
                        sum_values(*unit_of(a, s - 3))
                    project(a, 9 * s, 5)
                    transposes(a, s, 0)
                    turn_probs(a, s)
                    project(a, 9 * s + 5, 4)
                    first_out_projection(a, s)
                    transposes(a, s, 1)

            pe.wait_ge(ident_ready, 1)
            pe.wait_ge(ident_r_ready, 1)
            body(before[0])
            iterations(pe, body)

        @block.scalar
        def _(act):
            def split_stage(w):
                src, hi, _ = stage_parts(w)
                act.wait_ge(stage_loaded[w % 4], stage_count(w))
                nc.scalar.activation(hi, src, ACT.Copy).then_inc(weight_hi, 1)

            def split_wo(w):
                act.wait_ge(shared.wo_loaded[w % 4], DMA * (w // 4 + 1))
                act.wait_ge(projected, 3 * BATCHES - 2 + w // 4)
                nc.scalar.activation(shared.wo_part(w, 0), shared.wo_stage(w)[:, :].rearrange("p (k n) -> p k n", k=2),
                                     ACT.Copy).then_inc(shared.wo_hi, 1)

            def take_turned(a, s, late):
                f = fill_in(a, s, late)
                if f is None:
                    return
                kind, b, part = f
                if kind in "qk" and part % 2:
                    return
                need(act, turned[kind], count(*f))
                ps = turn_bank(s, 2 * late)
                if kind == "k":
                    if b.at(0):
                        act.wait_ge(kd_zeroed, 4)
                    need(act, scored, b.n * UNITS - UNITS)
                    for h in range(2):
                        rows = slice(h * 2 * DH, (h + 1) * 2 * DH)
                        ins = nc.scalar.activation(
                            kD[b.par][0][rows, :, h, :],
                            ps[rows, :].rearrange("p (c k) -> p c k", c=4), ACT.Copy)
                    ins.then_inc(kD_by_act, 1)
                elif kind == "q":
                    half = part // 2
                    need(act, scored, b.n * UNITS - UNITS + 4 * half + 2)
                    nc.scalar.activation(flat(qT[:, half, 0:4, :]), ps[:, :], ACT.Copy).then_inc(qT_by_act, 1)

            def x_highs(b, part):
                if not b.exists():
                    return
                need(act, xn_ready, b.n + 1)
                need(act, projected, b.n * 3)
                nc.scalar.activation(flat(xT[0][:, 4 * part:4 * part + 4, :]), xt_raw[b.par][:, raw_part(part)],
                                     ACT.Copy).then_inc(hi_ready["x"], 1)

            def context_highs(b, part):
                if not b.exists():
                    return
                need(act, c_loaded[b.par], (b.earlier + 1) * DMA)
                need(act, projected, b.n * 3 - 2)
                nc.scalar.activation(flat(ctxT[0][:, 4 * part:4 * part + 4, :]), c_raw[b.par][:, raw_part(part)],
                                     ACT.Copy).then_inc(hi_ready["c"], 1)

            def query_highs(b, half):
                if not b.exists():
                    return
                need(act, drained, b.n * 3 + half + 2)
                need(act, turned["q"], b.n * 4 - 2 + 2 * half)
                nc.scalar.activation(q_halves[:, half, :, 0, :],
                                     flat(q_sb[:, half:half + 1]).rearrange("p (q d) -> p q d", d=DH),
                                     ACT.Copy).then_inc(q_hi_ready, 1)

            def key_highs(b):
                if not b.exists():
                    return
                need(act, keys_drained, b.n + 1)
                need(act, turned["k"], b.n * 2)
                nc.scalar.activation(k_twice[0][:, :, :, :], twice(k_sb), ACT.Copy).then_inc(k_hi_ready, 1)

            def exponentials(b, s):
                if not b.exists():
                    return
                need(act, neg_max_ready, b.n * UNITS + s + 1)
                need(act, probs_turned, b.n * UNITS + s - 3)
                for q in range(4):
                    ins = nc.scalar.activation(probs[s % 4][:, q, :], score_ps[s % 2][:, q * P:(q + 1) * P],
                                               ACT.Exp, bias=neg_max[:, s, q:q + 1], scale=SCALE,
                                               accum_out=row_sum[:, s, q:q + 1])
                ins.then_inc(exp_done, 1)

            def copy_probsT(a, slot):
                b, s = unit_of(a, slot - 2)
                if not b.exists() or s % 2:
                    return
                need(act, probs_turned, b.n * UNITS + s + 1)
                need(act, values_summed, b.n * UNITS + s - 1)
                nc.scalar.activation(flat(probsT[0][:, :, :]), turn_bank(slot, 1)[:, :],
                                     ACT.Copy).then_inc(probsT_ready[0], 1)

            def body(a):
                for s in range(UNITS):
                    take_turned(a, s - 1, 1)
                    exponentials(a, s)
                    take_turned(a, s, 0)
                    copy_probsT(a, s)
                    if s in context_slots(a, False):
                        context_highs(a + 2, context_slots(a, False).index(s))
                    if s in X_SLOTS:
                        x_highs(a + 2, X_SLOTS.index(s))
                    if s == 1:
                        key_highs(a + 1)
                    if s == 4:
                        query_highs(a + 1, 0)
                    if s == 7:
                        query_highs(a + 1, 1)
                    for w in stages_in(a, s):
                        split_stage(w)
                    w = split_in(a, s, 0)
                    if w is not None:
                        split_wo(w)
                    if late_slot(a, s) in AT_HI:
                        act.wait_ge(projected, 3 * BATCHES)
                        shared.high_at(act, Batch(AT_HI.index(late_slot(a, s))))

            body(before[0])
            body(before[1])
            act.wait_ge(shared.gates_loaded, 2 * DMA)
            nc.scalar.activation(shared.tanhs[:, :], shared.gates[:, :], ACT.Tanh).then_inc(shared.gates_ready, 1)
            iterations(act, body, before[2:])

        @block.vector
        def _(dve):
            def split_stage(w):
                src, hi, lo = stage_parts(w)
                dve.wait_ge(weight_hi, w + 1)
                nc.vector.tensor_tensor(lo, src, hi, ALU.subtract).then_inc(weight_lo, 1)

            def split_wo(w):
                dve.wait_ge(shared.wo_hi, w + 1)
                nc.vector.tensor_tensor(shared.wo_part(w, 1), shared.wo_stage(w)[:, :].rearrange("p (k n) -> p k n", k=2),
                                        shared.wo_part(w, 0), ALU.subtract).then_inc(shared.wo_lo, 1)

            def take_turned(a, s, late):
                f = fill_in(a, s, late)
                if f is None:
                    return
                kind, b, part = f
                if kind in "qk" and part % 2 == 0:
                    return
                ps = turn_bank(s, 2 * late)
                if kind == "k":
                    need(dve, turned["k"], count(*f))
                    need(dve, scored, b.n * UNITS - UNITS)
                    for h in range(2):
                        rows = slice(h * 2 * DH, (h + 1) * 2 * DH)
                        ins = nc.vector.tensor_copy(
                            kD[b.par][1][rows, :, h, :],
                            ps[rows, :].rearrange("p (c k) -> p c k", c=4))
                    ins.then_inc(kD_by_dve, 1)
                elif kind == "q":
                    half = part // 2
                    need(dve, turned["q"], count(*f))
                    need(dve, scored, b.n * UNITS - UNITS + 4 * half + 4)
                    nc.vector.tensor_copy(flat(qT[:, half, 4:8, :]), ps[:, :]).then_inc(qT_by_dve, 1)

            def x_lows(b, part):
                if not b.exists():
                    return
                need(dve, hi_ready["x"], count("x", b, part))
                hi, lo = (flat(t[:, 4 * part:4 * part + 4, :]) for t in xT)
                nc.vector.tensor_tensor(lo, xt_raw[b.par][:, raw_part(part)], hi,
                                        ALU.subtract).then_inc(lo_ready["x"], 1)

            def context_lows(b, part):
                if not b.exists():
                    return
                need(dve, hi_ready["c"], count("c", b, part))
                hi, lo = (flat(t[:, 4 * part:4 * part + 4, :]) for t in ctxT)
                nc.vector.tensor_tensor(lo, c_raw[b.par][:, raw_part(part)], hi,
                                        ALU.subtract).then_inc(lo_ready["c"], 1)

            def drain_keys(b):
                if not b.exists():
                    return
                need(dve, projected, b.n * 3 + 1)
                need(dve, k_lo_ready, b.n)
                nc.vector.tensor_tensor(k_sb[:, :], mm_bank(b, 0)[:, 0:KVD], bkv_row[:, 0:KVD],
                                        ALU.add).then_inc(keys_drained, 1)

            def drain(b, g):
                if not b.exists():
                    return
                need(dve, projected, b.n * 3 + g + 1)
                ps = mm_bank(b, g)
                if g == 0:
                    need(dve, values_summed, b.n * UNITS - UNITS)
                    ins = nc.vector.tensor_tensor(values[b.par][:, :], ps[:, KVD:], bkv_row[:, KVD:], ALU.add)
                else:
                    half = g - 1
                    if b.at(0):
                        dve.wait_ge(bq_loaded, DMA)
                    need(dve, q_lo_ready, b.n * 2 - 1 + half)
                    order = "p (q j d) -> p q j d"
                    ins = nc.vector.tensor_tensor(
                        q_sb[:, half].rearrange("p j (q d) -> p q j d", d=DH),
                        ps[:, :].rearrange(order, q=4, j=GROUPS),
                        bq_row[:, half * HALF:(half + 1) * HALF].rearrange(order, q=4, j=GROUPS), ALU.add)
                ins.then_inc(drained, 1)

            def maxima(b, s):
                if not b.exists():
                    return
                need(dve, scored, b.n * UNITS + s + 1)
                nc.vector.tensor_reduce(row_max[:, s, :], score_ps[s % 2][:, :].rearrange("p (q k) -> p q k", q=4),
                                        AX_X, ALU.max).then_inc(row_max_ready, 1)
                need(dve, row_max_ready, b.n * UNITS + s + 1)
                nc.vector.tensor_scalar(neg_max[:, s, :], row_max[:, s, :], -SCALE, None,
                                        ALU.mult).then_inc(neg_max_ready, 1)

            def inverse_sums(b, s):
                if not b.exists():
                    return
                need(dve, exp_done, b.n * UNITS + s + 1)
                nc.vector.reciprocal(inv_sum[:, s, :], row_sum[:, s, :]).then_inc(inv_ready, 1)

            def copy_probsT(a, slot):
                b, s = unit_of(a, slot - 2)
                if not b.exists() or s % 2 == 0:
                    return
                need(dve, probs_turned, b.n * UNITS + s + 1)
                need(dve, values_summed, b.n * UNITS + s - 1)
                nc.vector.tensor_copy(flat(probsT[1][:, :, :]), turn_bank(slot, 1)[:, :]).then_inc(probsT_ready[1], 1)

            def copy_at(b, s):
                half, j = divmod(s, GROUPS)
                if not b.exists() or j < GROUPS - 1:
                    return
                need(dve, values_summed, b.n * UNITS + s + 1)
                if half == 0:
                    need(dve, at_stored[b.par], b.earlier * DMA)
                nc.vector.tensor_copy(at_sb[b.par][:, half * HALF:(half + 1) * HALF],
                                      at_ps[:, :]).then_inc(at_ready, 1)

            def row_stats(b):
                if not b.exists():
                    return
                need(dve, x_loaded, (b.n + 1) * DMA)
                for h in range(2):
                    nc.vector.bn_stats(stats[:, h, :], x_nat[:, h * HALF:(h + 1) * HALF]).then_inc(stats_ready, 1)

            def variance(b):
                if not b.exists():
                    return
                nc.vector.bn_aggr(mean_var[:, :], flat(stats[:, :, :])).then_inc(mean_ready, 1)
                need(dve, mean_ready, b.n + 1)
                nc.vector.tensor_scalar(var_eps[:, :], mean_var[:, 1:2], EPS, None, ALU.add).then_inc(var_ready, 1)

            def before_variance(b):
                need(dve, stats_ready, b.n * 2 + 2)
                need(dve, moments_stored, b.n * DMA)

            def centre(b):
                if not b.exists():
                    return
                need(dve, xt_loaded[b.par], (b.earlier + 1) * DMA)
                need(dve, moments_loaded[b.par], (b.earlier + 1) * DMA)
                t = xt_raw[b.par][:, :].rearrange("p (k t) -> p k t", k=KC)
                mean = moments[b.par][:, :, 0].unsqueeze(1).broadcast_to([P, KC, P])
                nc.vector.tensor_tensor(t, t, mean, ALU.subtract).then_inc(x_centred, 1)

            def scale(b):
                if not b.exists():
                    return
                need(dve, x_centred, b.n + 1)
                t = xt_raw[b.par][:, :].rearrange("p (k t) -> p k t", k=KC)
                rstd = moments[b.par][:, :, 1].unsqueeze(1).broadcast_to([P, KC, P])
                nc.vector.tensor_tensor(t, t, rstd, ALU.mult).then_inc(xn_ready, 1)

            def body(a):
                for s in range(UNITS):
                    if s == stats_slot(a) + 1 and (a + 3).exists():
                        before_variance(a + 3)
                    maxima(a, s)
                    if s == 2:
                        drain(a + 1, 0)
                    take_turned(a, s - 1, 1)
                    inverse_sums(*unit_of(a, s - 1))
                    if s == stats_slot(a) + 1:
                        variance(a + 3)
                    copy_at(*unit_of(a, s - 3))
                    if s == 0:
                        drain_keys(a + 1)
                    if s == 6:
                        drain(a + 1, 2)
                    take_turned(a, s, 0)
                    copy_probsT(a, s)
                    if s == 3:
                        drain(a + 1, 1)
                    if s in context_slots(a, True):
                        context_lows(a + 2, context_slots(a, True).index(s))
                    if s == centre_slot(a):
                        centre(a + 2)
                    if s == SCALE_SLOT:
                        scale(a + 2)
                    if s in X_SLOTS:
                        x_lows(a + 2, X_SLOTS.index(s))
                    if s == stats_slot(a):
                        row_stats(a + 3)
                    for w in stages_in(a, s):
                        split_stage(w)
                    w = split_in(a, s, 1)
                    if w is not None:
                        split_wo(w)
                    if late_slot(a, s) == BO_SLOT:
                        dve.wait_ge(shared.gates_ready, 1)
                        dve.wait_ge(bo_loaded, DMA)
                        nc.vector.tensor_scalar(shared.bo_row[:, :], shared.bo_row[:, :], shared.tanhs[:, 0:1], None,
                                                ALU.mult).then_inc(shared.bo_scaled, 1)
                    if late_slot(a, s) in AT_LO:
                        shared.low_at(dve, nc.vector, Batch(AT_LO.index(late_slot(a, s))))

            def adapter_masks():
                dve.wait_ge(starts_loaded, DMA)
                dve.wait_ge(batch_ready, 2)
                nc.vector.tensor_copy(starts_f[:, :], starts_i[:, :]).then_inc(mask_steps, 1)
                nc.vector.tensor_copy(batch_f[:, :], batch_i[:, :]).then_inc(mask_steps, 1)
                nc.vector.tensor_copy(shared.row_f[:, :], row_i[:, :]).then_inc(mask_steps, 1)
                dve.wait_ge(mask_steps, 3)
                nc.vector.tensor_scalar(begun[:, :], batch_f[:, :], starts_f[:, 0:1], None, ALU.is_ge).then_inc(mask_steps, 1)
                for k in range(1, ADAPTERS + 1):
                    dve.wait_ge(mask_steps, 3 + k)
                    nc.vector.scalar_tensor_tensor(out=begun[:, :], in0=batch_f[:, :], scalar=starts_f[:, k:k + 1],
                                                   in1=begun[:, :], op0=ALU.is_ge, op1=ALU.add).then_inc(mask_steps, 1)
                dve.wait_ge(mask_steps, 4 + ADAPTERS)
                nc.vector.tensor_scalar(begun_at[:, :], shared.row_f[:, :], float(RANK), 2.0, ALU.is_ge, ALU.add).then_inc(mask_steps, 1)
                steps = 5 + ADAPTERS
                for at_row, by in ((2 * RANK, 1.0), (LO_ROW, -2.0), (LO_ROW + RANK, 1.0), (LO_ROW + 2 * RANK, 1.0)):
                    dve.wait_ge(mask_steps, steps)
                    nc.vector.tensor_scalar(row_step[:, :], shared.row_f[:, :], float(at_row), by, ALU.is_ge,
                                            ALU.mult).then_inc(mask_steps, 1)
                    dve.wait_ge(mask_steps, steps + 1)
                    nc.vector.tensor_tensor(begun_at[:, :], begun_at[:, :], row_step[:, :], ALU.add).then_inc(mask_steps, 1)
                    steps += 2
                dve.wait_ge(mask_steps, steps)
                nc.vector.tensor_scalar(shared.mask[:, :], begun[:, :], float(ADAPTERS + 1), begun_at[:, 0:1], ALU.min,
                                        ALU.is_equal).then_inc(mask_steps, 1)
                dve.wait_ge(mask_steps, steps + 1)

            adapter_masks()
            dve.wait_ge(ident_ready, 1)
            nc.vector.tensor_copy(ident_r[:, :], ident[:, :]).then_inc(ident_r_ready, 1)
            row_stats(Batch(0))
            before_variance(Batch(0))
            variance(Batch(0))
            body(before[0])
            dve.wait_ge(kd_zeroed, 4)
            dve.wait_ge(biases_loaded, 2 * DMA)
            body(before[1])
            iterations(dve, body, before[2:])

        @block.gpsimd
        def _(pool):
            nc.gpsimd.iota(batch_i[:, :], pattern=[[1, BATCHES]], base=0, channel_multiplier=0).then_inc(batch_ready, 1)
            nc.gpsimd.iota(row_i[:, :], pattern=[[0, 1]], base=0, channel_multiplier=1).then_inc(batch_ready, 1)
            nc.gpsimd.memset(ident[:, :], 0.0).then_inc(ident_zeroed, 1)
            nc.gpsimd.memset(minus_half[:, :], -0.5).then_inc(ident_zeroed, 1)
            pool.wait_ge(ident_zeroed, 2)
            nc.gpsimd.affine_select(out=ident[:, :], in_=ident[:, :], compare_op=ALU.not_equal, fill=1.0,
                                    base=0, pattern=[[-1, P]], channel_multiplier=1).then_inc(ident_ready, 1)
            for i in range(2):
                for t in kD[i]:
                    nc.gpsimd.memset(t[:, :, :, :].bitcast(F32), 0.0).then_inc(kd_zeroed, 1)

            def inverse_std(b):
                if not b.exists():
                    return
                need(pool, var_ready, b.n + 1)
                nc.gpsimd.tensor_tensor(mean_var[:, 1:2], var_eps[:, :], minus_half[:, :], ALU.pow).then_inc(rstd_ready, 1)

            def divide(b, s):
                if not b.exists():
                    return
                need(pool, inv_ready, b.n * UNITS + s + 1)
                nc.gpsimd.tensor_tensor(probs[s % 4][:, :, :], probs[s % 4][:, :, :],
                                        inv_sum[:, s, :].unsqueeze(2).broadcast_to([P, 4, P]),
                                        ALU.mult).then_inc(probs_ready, 1)

            def query_lows(b, half):
                if not b.exists():
                    return
                need(pool, q_hi_ready, b.n * 2 + half + 1)
                nc.gpsimd.tensor_tensor(q_halves[:, half, :, 1, :],
                                        flat(q_sb[:, half:half + 1]).rearrange("p (q d) -> p q d", d=DH),
                                        q_halves[:, half, :, 0, :], ALU.subtract).then_inc(q_lo_ready, 1)

            def key_lows(b):
                if not b.exists():
                    return
                need(pool, k_hi_ready, b.n + 1)
                nc.gpsimd.tensor_tensor(k_twice[1][:, :, :, :], twice(k_sb), k_twice[0][:, :, :, :],
                                        ALU.subtract).then_inc(k_lo_ready, 1)

            def body(a):
                for s in range(UNITS):
                    divide(*unit_of(a, s - 1))
                    if s == 2:
                        key_lows(a + 1)
                    if s == stats_slot(a) + 1:
                        inverse_std(a + 3)
                    if s == 4:
                        query_lows(a + 1, 0)
                    if s == 7:
                        query_lows(a + 1, 1)
                    t = late_slot(a, s)
                    if t in BIAS_X:
                        if t == BIAS_X[0]:
                            pool.wait_ge(shared.bo_scaled, 1)
                        shared.bias_x(pool, Batch(BIAS_X.index(t)))

            inverse_std(Batch(0))
            body(before[0])
            iterations(pool, body)


def ffn_phase(nc, shared, w_t, bias, lora_a_t, lora_b_t, out):
    with ExitStack() as ctx:
        def sb(name, shape, dt=F32):
            return ctx.enter_context(nc.sbuf_tensor(name, shape, dt))

        def sem(name):
            return ctx.enter_context(nc.semaphore(name))

        bank, o_ps = shared.bank, shared.o_ps
        f_ps, turn_ps, u_ps = bank[2:4], bank[4:6], bank[6:8]

        ident, minus_half, tanhs, x_in = shared.ident, shared.minus_half, shared.tanhs, shared.raw_x
        wf_right = [sb(f"wf_right_{t}", [P, KC, HALF], F32R) for t in ("hi", "lo")]
        wfs = [[t[:, :, HALF:EMBED] for t in shared.wide], [t[:, :, :] for t in wf_right]]
        lb_hi = sb("lb_hi", [STACK, EMBED], F32R)
        lb_lo = sb("lb_lo", [LR + 1, EMBED], F32R)
        la = sb("la", [P, KC, LR])
        x1 = [sb(f"x1_{i}", [P, EMBED]) for i in range(2)]
        x2T = [sb(f"x2T_{t}", [P, KC, P], F32R) for t in ("hi", "lo")]
        x2T_full = sb("x2T_full", [P, KC, P])
        out_sb = shared.result
        spare = sb("spare", [P, EMBED])
        mask = shared.mask
        odd = sb("u_odd", [LR, P])
        u_odd, u_sum = odd[:, :], u_ps[0][0:LR, P:2 * P]
        uT = sb("uT", [STACK, P], F32R)
        stats = sb("stats2", [P, 2, 6])
        mean_var = sb("mean_var2", [P, 2])
        var_eps = sb("var_eps2", [P, 1])
        rstd = sb("rstd2", [P, 1])

        stage_loaded = [sem(f"wf_stage_loaded{i}") for i in range(4)]
        la_loaded = sem("la_loaded")
        lb_zeroed, lb_loaded, lb_hi_ready, lb_lo_ready = (sem(n) for n in ("lb_zeroed", "lb_loaded", "lb_hi_ready", "lb_lo_ready"))
        stack_set = sem("stack_set")
        weight_hi, weight_lo = sem("w_hi"), [sem("w_lo_by_dve"), sem("w_lo_by_pool")]
        o_done, x1_ready = shared.o_done, shared.x1_ready
        stats_ready, mean_ready, var_ready, rstd_ready, x2_ready = (
            sem(n) for n in ("stats_ready2", "mean_ready2", "var_ready2", "rstd_ready2", "x2_ready"))
        x2_turned, x2_hi, x2_full, x2_lo = sem("x2_turned"), sem("x2_hi"), sem("x2_full"), sem("x2_lo")
        u_done, u_odd_ready, u_ready, u_hi, u_lo = (
            sem(n) for n in ("u_done", "u_odd_ready", "u_ready", "u_hi", "u_lo"))
        f_done, out_ready = sem("f_done"), sem("out_ready")
        out_stored = [sem(f"out_stored{i}") for i in range(2)]

        stage_tiles = shared.raw_c + [out_sb[1], spare]
        lb_stage = x1[1][:, :]

        def stage(w):
            return stage_tiles[w % 4][:, :].rearrange("p (k n) -> p k n", k=2)

        def weight_part(w, t):
            k = 2 * (w % 4)
            return wfs[w // 4][t][:, k:k + 2, :]

        def wait_weight_lo(engine, w):
            engine.wait_ge(weight_lo[w % 2], w // 2 + 1)

        loop_pairs = 14
        after = [Batch(a) for a in range(2 * loop_pairs + 1, BATCHES)]

        def iterations(engine, body):
            body(Batch(0))
            with engine.Fori(0, loop_pairs) as pair:
                body(Batch(1, pair))
                body(Batch(2, pair))
            for i in after:
                body(i)

        block = ctx.enter_context(nc.Block())

        @block.sync
        def _(sp):
            w_v = w_t.rearrange("(k p) n -> p k n", p=P)

            def load_stage(w):
                k, cols = 2 * (w % 4), slice(w // 4 * HALF, (w // 4 + 1) * HALF)
                if w >= 4:
                    wait_weight_lo(sp, w - 4)
                sp.dma_start(stage(w), w_v[:, k:k + 2, cols]).then_inc(stage_loaded[w % 4], DMA)

            for w in (0, 1, 3):
                load_stage(w)
            sp.dma_start(la[:, :, :], lora_a_t.rearrange("(k p) r -> p k r", p=P)).then_inc(la_loaded, DMA)
            sp.wait_ge(lb_zeroed, 1)
            sp.dma_start(lb_stage[0:LR, :], lora_b_t).then_inc(lb_loaded, DMA)
            sp.dma_start(lb_stage[LR:LR + 1, :], bias.unsqueeze(0)).then_inc(lb_loaded, DMA)
            sp.dma_start(lb_stage[LO_ROW:STACK, :], lora_b_t).then_inc(lb_loaded, DMA)
            sp.wait_ge(shared.at_stored[1], DMA * (BATCHES // 2))
            for w in (2, 4, 5, 6, 7):
                load_stage(w)

            def body(i):
                if i.at(-1):
                    for w in (4, 5):
                        wait_weight_lo(sp, w)
                if (i + 3).exists():
                    shared.load_at(sp, i + 3)
                    shared.load_x_in(sp, i + 3)
                if i.exists():
                    need(sp, out_ready, i.n * 2 + 2)
                    sp.dma_start(out[i.n], out_sb[i.par][:, :]).then_inc(out_stored[i.par], DMA)

            body(Batch(-1))
            iterations(sp, body)
            for i in range(2):
                sp.wait_ge(out_stored[i], DMA * (BATCHES // 2))

        @block.tensor
        def _(pe):
            def out_projection(b, g):
                if not b.exists():
                    return
                need(pe, shared.at_lo, b.n + 1)
                need(pe, x1_ready, b.n * 2 + g - 1)
                for r in range(GROUP_MM):
                    mm = shared.out_matmul(b, g, r)
                mm.then_inc(o_done, 1)

            def feed_forward(b, g):
                if not b.exists():
                    return
                need(pe, x2_lo, b.n * 2 + 2)
                need(pe, out_ready, b.n * 2 + g - 1)
                for r in range(GROUP_MM):
                    k, term = divmod(r, TERMS)
                    if b.at(0) and r % (2 * TERMS) == 0:
                        wait_weight_lo(pe, g * KC // 2 + r // (2 * TERMS))
                    nc.tensor.matmul(f_ps[g][:, :], x2T[term // 2][:, k, :], wfs[g][term % 2][:, k, :],
                                     start=(r == 0), stop=False)
                if b.at(0):
                    pe.wait_ge(lb_lo_ready, 1)
                need(pe, u_lo, b.n + 1)
                cols = slice(g * HALF, (g + 1) * HALF)
                nc.tensor.matmul(f_ps[g][:, :], uT[:, :], lb_hi[:, cols], start=False, stop=False)
                nc.tensor.matmul(f_ps[g][:, :], uT[0:LR + 1, :], lb_lo[:, cols], start=False,
                                 stop=True).then_inc(f_done, 1)

            def turn_x2(b):
                if not b.exists():
                    return
                need(pe, x2_ready, b.n + 1)
                for f in range(2):
                    need(pe, x2_lo, b.n * 2 + f - 1)
                    need(pe, x2_full, b.n * 2 + f - 1)
                    for i in range(4):
                        k = 4 * f + i
                        mm = nc.tensor.transpose(turn_ps[f][:, i * P:(i + 1) * P],
                                                 out_sb[b.par][:, k * P:(k + 1) * P], ident[:, :])
                    mm.then_inc(x2_turned, 1)

            def lora_down(b):
                if not b.exists():
                    return
                if b.at(0):
                    pe.wait_ge(la_loaded, DMA)
                need(pe, x2_full, b.n * 2 + 2)
                need(pe, u_lo, b.n)
                for k in range(KC):
                    row = LO_ROW * (k % 2)
                    mm = nc.tensor.matmul(u_ps[k % 2][row:row + LR, 0:P], la[:, k, :], x2T_full[:, k, :],
                                          start=(k < 2), stop=(k >= KC - 2))
                mm.then_inc(u_done, 1)

            def body(i):
                if i.exists():
                    out_projection(i + 1, 1)
                lora_down(i)
                feed_forward(i, 0)
                feed_forward(i, 1)
                out_projection(i + 2, 0)
                turn_x2(i + 1)

            body(Batch(-1))
            iterations(pe, body)

        @block.scalar
        def _(act):
            def high_x2(b):
                if not b.exists():
                    return
                need(act, f_done, b.n * 2)
                need(act, u_done, b.n)
                for f in range(2):
                    need(act, x2_turned, b.n * 2 + f + 1)
                    part = slice(4 * f, 4 * f + 4)
                    nc.scalar.activation(x2T[0][:, part, :].rearrange("p k t -> p (k t)"), turn_ps[f][:, :],
                                         ACT.Copy).then_inc(x2_hi, 1)
                    nc.scalar.activation(x2T_full[:, part, :].rearrange("p k t -> p (k t)"), turn_ps[f][:, :],
                                         ACT.Copy).then_inc(x2_full, 1)

            def body(i):
                if (i + 2).exists():
                    shared.high_at(act, i + 2)
                high_x2(i + 1)

            def split_stage(w):
                act.wait_ge(stage_loaded[w % 4], DMA * (w // 4 + 1))
                nc.scalar.activation(weight_part(w, 0), stage(w), ACT.Copy).then_inc(weight_hi, 1)

            for w in range(2):
                split_stage(w)
            high_x2(Batch(0))
            for w in range(2, 4):
                split_stage(w)
            act.wait_ge(lb_loaded, 3 * DMA)
            nc.scalar.activation(lb_hi[:, :], lb_stage[0:STACK, :], ACT.Copy).then_inc(lb_hi_ready, 1)
            for w in range(4, KC):
                split_stage(w)
            iterations(act, body)

        @block.vector
        def _(dve):

            def split_stage(w):
                dve.wait_ge(weight_hi, w + 1)
                nc.vector.tensor_tensor(weight_part(w, 1), stage(w), weight_part(w, 0),
                                        ALU.subtract).then_inc(weight_lo[0], 1)

            def attended(b, g):
                if not b.exists():
                    return
                cols = slice(g * HALF, (g + 1) * HALF)
                need(dve, o_done, b.n * 2 + g + 1)
                need(dve, shared.x_biased, b.n + 1)
                need(dve, out_ready, b.n * 2 - 2)
                nc.vector.scalar_tensor_tensor(out=x1[b.par][:, cols], in0=o_ps[g][:, :], scalar=tanhs[:, 0:1],
                                               in1=x_in[b.par][:, cols], op0=ALU.mult,
                                               op1=ALU.add).then_inc(x1_ready, 1)

            def norm(b):
                if not b.exists():
                    return
                for h in range(2):
                    need(dve, x1_ready, b.n * 2 + h + 1)
                    nc.vector.bn_stats(stats[:, h, :], x1[b.par][:, h * HALF:(h + 1) * HALF]).then_inc(stats_ready, 1)
                dve.wait_ge(shared.bo_scaled, 1)
                need(dve, stats_ready, b.n * 2 + 2)
                nc.vector.bn_aggr(mean_var[:, :], stats[:, :, :].rearrange("p h s -> p (h s)")).then_inc(mean_ready, 1)
                need(dve, mean_ready, b.n + 1)
                nc.vector.tensor_scalar(var_eps[:, :], mean_var[:, 1:2], EPS, None, ALU.add).then_inc(var_ready, 1)
                if b.at(0):
                    for i in range(2):
                        dve.wait_ge(shared.at_stored[i], DMA * (BATCHES // 2))
                need(dve, rstd_ready, b.n + 1)
                need(dve, out_stored[b.par], b.earlier * DMA)
                nc.vector.tensor_scalar(out_sb[b.par][:, :], x1[b.par][:, :], mean_var[:, 0:1], rstd[:, 0:1],
                                        ALU.subtract, ALU.mult).then_inc(x2_ready, 1)

            def outputs(b, g):
                if not b.exists():
                    return
                cols = slice(g * HALF, (g + 1) * HALF)
                need(dve, f_done, b.n * 2 + g + 1)
                nc.vector.scalar_tensor_tensor(out=out_sb[b.par][:, cols], in0=f_ps[g][:, :], scalar=tanhs[:, 1:2],
                                               in1=x1[b.par][:, cols], op0=ALU.mult,
                                               op1=ALU.add).then_inc(out_ready, 1)

            def low_x2(b):
                if not b.exists():
                    return
                for f in range(2):
                    need(dve, x2_full, b.n * 2 + f + 1)
                    hi, lo = (t[:, 4 * f:4 * f + 4, :].rearrange("p k t -> p (k t)") for t in x2T)
                    nc.vector.tensor_tensor(lo, turn_ps[f][:, :], hi, ALU.subtract).then_inc(x2_lo, 1)

            def split_u(b):
                if not b.exists():
                    return
                need(dve, u_done, b.n + 1)
                nc.vector.tensor_scalar(u_odd, u_ps[1][LO_ROW:STACK, 0:P], mask[LO_ROW:STACK, bass.ds(b.n, 1)], None,
                                        ALU.mult).then_inc(u_odd_ready, 1)
                need(dve, u_odd_ready, b.n + 1)
                nc.vector.scalar_tensor_tensor(out=u_sum, in0=u_ps[0][0:LR, 0:P], scalar=mask[0:LR, bass.ds(b.n, 1)],
                                               in1=u_odd, op0=ALU.mult, op1=ALU.add).then_inc(u_ready, 1)
                need(dve, u_ready, b.n + 1)
                need(dve, f_done, b.n * 2)
                nc.vector.tensor_copy(uT[0:LR, :], u_sum).then_inc(u_hi, 1)
                need(dve, u_hi, b.n + 1)
                nc.vector.tensor_tensor(uT[LO_ROW:STACK, :], u_sum, uT[0:LR, :], ALU.subtract).then_inc(u_lo, 1)

            def body(i):
                attended(i + 1, 1)
                split_u(i)
                if i.at(0):
                    for w in (4, 6):
                        split_stage(w)
                    wait_weight_lo(dve, 6)
                norm(i + 1)
                outputs(i, 0)
                outputs(i, 1)
                attended(i + 2, 0)
                low_x2(i + 1)

            attended(Batch(0), 0)
            attended(Batch(0), 1)
            norm(Batch(0))
            nc.vector.tensor_scalar(uT[LO_ROW // 2:LO_ROW, :],
                                    shared.row_f[LO_ROW // 2:LO_ROW, 0:1].broadcast_to([LO_ROW // 2, P]), float(LR), None,
                                    ALU.is_equal).then_inc(stack_set, 1)
            split_stage(0)
            low_x2(Batch(0))
            split_stage(2)
            dve.wait_ge(lb_hi_ready, 1)
            nc.vector.tensor_tensor(lb_lo[:, :], lb_stage[0:LR + 1, :], lb_hi[0:LR + 1, :],
                                    ALU.subtract).then_inc(lb_lo_ready, 1)
            dve.wait_ge(lb_lo_ready, 1)
            attended(Batch(1), 0)
            iterations(dve, body)

        @block.gpsimd
        def _(pool):
            nc.gpsimd.memset(lb_stage, 0.0).then_inc(lb_zeroed, 1)
            def inverse_std(b):
                if not b.exists():
                    return
                need(pool, var_ready, b.n + 1)
                nc.gpsimd.tensor_tensor(rstd[:, :], var_eps[:, :], minus_half[:, :], ALU.pow).then_inc(rstd_ready, 1)

            def body(i):
                inverse_std(i + 1)
                if (i + 2).exists():
                    shared.low_at(pool, nc.gpsimd, i + 2)
                    shared.bias_x(pool, i + 2)

            def split_stage(w):
                pool.wait_ge(weight_hi, w + 1)
                nc.gpsimd.tensor_tensor(weight_part(w, 1), stage(w), weight_part(w, 0),
                                        ALU.subtract).then_inc(weight_lo[1], 1)

            inverse_std(Batch(0))
            for w in range(1, KC, 2):
                split_stage(w)
            iterations(pool, body)


def build_program(nc, x, x_t, ctx_in, g_xattn, g_ffn, wq, bq, wk, bk, wv, bv, wo, bo, w_t, bias, lora_a_t, lora_b_t,
                  starts, out):
    at_dram = nc.dram_tensor("attention_out", (BATCHES, P, EMBED), F32).ap()
    with ExitStack() as ctx:
        shared = Shared(nc, ctx, x, at_dram)
        attention_phase(nc, shared, x, x_t, ctx_in, g_xattn, g_ffn, wq, bq, wk, bk, wv, bv, wo, bo, starts, at_dram)
        ffn_phase(nc, shared, w_t, bias, lora_a_t, lora_b_t, out)


def kernel(x, ctx_4096, g_xattn, g_ffn, L0_xattn_Wq, L0_xattn_bq, L0_xattn_Wk, L0_xattn_bk, L0_xattn_Wv,
           L0_xattn_bv, L0_xattn_Wo, L0_xattn_bo, L0_ffn_weight, L0_ffn_bias, L0_ffn_lora_A, L0_ffn_lora_B,
           L0_ffn_lora_start_indices):
    import numpy as np
    import concourse.bacc as bacc
    from concourse.bass_utils import run_bass_kernel_spmd

    nc = bacc.Bacc("TRN2", target_bir_lowering=False, num_devices=1)
    lora_b = np.asarray(L0_ffn_lora_B)
    wo = np.asarray(L0_xattn_Wo).reshape(2, 4, GROUPS, DH, EMBED)
    ins = {
        "x": x, "x_t": x, "ctx": ctx_4096, "g_xattn": g_xattn, "g_ffn": g_ffn,
        "wq": L0_xattn_Wq, "bq": L0_xattn_bq, "wk": L0_xattn_Wk, "bk": L0_xattn_bk,
        "wv": L0_xattn_Wv, "bv": L0_xattn_bv, "wo": wo.transpose(0, 2, 1, 3, 4).reshape(EMBED, EMBED), "bo": L0_xattn_bo,
        "w_t": np.asarray(L0_ffn_weight).T, "bias": L0_ffn_bias,
        "lora_a_t": np.asarray(L0_ffn_lora_A).reshape(-1, EMBED).T,
        "lora_b_t": lora_b.transpose(0, 2, 1).reshape(-1, EMBED),
        "starts": L0_ffn_lora_start_indices,
    }
    for name, a in (("ctx", ctx_4096), ("x_t", x)):
        ins[name] = np.asarray(a).reshape(BATCHES, P, KC, P).transpose(0, 3, 2, 1).reshape(BATCHES, P, EMBED)
    arrays, args = {}, []
    for name, a in ins.items():
        a = np.ascontiguousarray(a)
        arrays[f"in_{name}"] = a
        args.append(nc.dram_tensor(f"in_{name}", a.shape, mybir.dt.from_np(a.dtype), kind="ExternalInput").ap())
    args.append(nc.dram_tensor("out_x", (BATCHES, P, EMBED), F32, kind="ExternalOutput").ap())
    build_program(nc, *args)
    r = run_bass_kernel_spmd(nc, [arrays], core_ids=[0])
    return r.results[0]["out_x"]
```
